# Optimizing a Trainium2 kernel written in Bass

```python
import numpy as np
import jax
import jax.numpy as jnp

def _softmax(x, axis=-1):
    return jax.nn.softmax(x, axis=axis)

def _gelu(x):
    return jax.nn.gelu(x, approximate=True)

def _silu(x):
    return jax.nn.silu(x)

def _sigmoid(x):
    return jax.nn.sigmoid(x)

def _layernorm(x, axis=-1, eps=1e-05):
    m = jnp.mean(x, axis=axis, keepdims=True)
    v = jnp.var(x, axis=axis, keepdims=True)
    return (x - m) / jnp.sqrt(v + eps)

def _scatter_add(tgt, idx, src, axis=0):
    return tgt.at[idx].add(src)

def _segment_sum(src, seg, n):
    return jax.ops.segment_sum(src, seg, n)
kernel_name = 'mk_adj_ffn_d1_adj_r2_23215c'

def setup_inputs(seed: int=0):
    np.random.seed(seed)
    _w = jnp.asarray

    def _rec_inputs():
        import jax
        import jax.numpy as jnp
        _gk = jax.random.key(seed)
        x = -0.0005207 + 1.001 * jax.random.normal(jax.random.fold_in(_gk, 1), (32, 256, 128), jnp.float32)
        _a = jax.random.bernoulli(jax.random.fold_in(_gk, 2), 0.0625, (32, 256, 256))
        _a = jnp.logical_or(_a, jnp.swapaxes(_a, -1, -2))
        _a = jnp.logical_or(_a, jnp.eye(256, dtype=bool))
        _af = _a.astype(jnp.float32)
        _af = _af * jax.random.uniform(jax.random.fold_in(_gk, 3), (32, 256, 256), jnp.float32, 0.05, 1)
        adj = _af
        return (x, adj)
    x, adj = _rec_inputs()

    def _L0_gnn_setup():
        import jax, jax.numpy as jnp
        import numpy as np
        EPS = 1e-07
        key = jax.random.key(seed)
        k1, k2, k3, k4, k5 = jax.random.split(key, 5)
        B, L, D, U = (8, 512, 128, 128)
        seq_data = jax.random.normal(k1, (B, L, D), dtype=jnp.float32)
        graph = jax.random.uniform(k2, (B, L, L), dtype=jnp.float32)
        scale = 1.0 / np.sqrt(D)
        e_weight = jax.random.normal(k3, (D, U), dtype=jnp.float32) * scale
        Wx = jax.random.normal(k4, (U, U), dtype=jnp.float32) * scale
        Wh = jax.random.normal(k5, (U, U), dtype=jnp.float32) * scale
        b = jnp.zeros((U,), dtype=jnp.float32)
        return {'seq_data': seq_data, 'graph': graph, 'e_weight': e_weight, 'Wx': Wx, 'Wh': Wh, 'b': b}
    _L0_gnn_all = _L0_gnn_setup()
    _L0_gnn_in = {k: v for k, v in _L0_gnn_all.items() if k in ('e_weight', 'Wx', 'Wh', 'b')}
    del _L0_gnn_all

    def _L0_ffn_setup():
        import jax, jax.numpy as jnp
        import numpy as np
        DIM = 128
        HEADS = 8
        NUM_KEYS = 128
        NUM_KV = NUM_KEYS ** 2
        PK_TOPK = 16
        FINAL_TOPK = 16
        DIM_KEY = DIM // 2
        P = 2

        def _pk(x, Wq_pk, pk_keys):
            b, n, _ = x.shape
            q = (x @ Wq_pk).reshape(b, n, P, HEADS, DIM_KEY).transpose(2, 0, 1, 3, 4)
            sim = jnp.einsum('pbnhd,pkhd->pbnhk', q, pk_keys)
            scores, idx = jax.lax.top_k(sim, PK_TOPK)
            idx0 = idx[0]
            idx1 = idx[1] * NUM_KEYS
            index = (idx0[..., :, None] + idx1[..., None, :]).reshape(b, n, HEADS, PK_TOPK * PK_TOPK)
            score = (scores[0][..., :, None] + scores[1][..., None, :]).reshape(b, n, HEADS, PK_TOPK * PK_TOPK)
            final_scores, pk_idx = jax.lax.top_k(score, FINAL_TOPK)
            final_indices = jnp.take_along_axis(index, pk_idx, axis=-1)
            final_scores = jax.nn.softmax(final_scores, axis=-1)
            return (final_scores, final_indices)
        key = jax.random.key(seed)
        ks = jax.random.split(key, 7)
        b, n = (2, 512)
        std = 0.02
        x = jax.random.normal(ks[0], (b, n, DIM), dtype=jnp.float32)
        Wq_pk = jax.random.normal(ks[1], (DIM, P * HEADS * DIM_KEY), dtype=jnp.float32) * std
        pk_keys = jax.random.normal(ks[2], (P, NUM_KEYS, HEADS, DIM_KEY), dtype=jnp.float32) * std
        Wq = jax.random.normal(ks[3], (DIM, HEADS * DIM), dtype=jnp.float32) * std
        keys_table = jax.random.normal(ks[4], (NUM_KV * HEADS, DIM), dtype=jnp.float32) * std
        values_table = jax.random.normal(ks[5], (NUM_KV * HEADS, DIM), dtype=jnp.float32) * std
        Wo = jax.random.normal(ks[6], (DIM * HEADS, DIM), dtype=jnp.float32) * std
        return {'x': x, 'Wq_pk': Wq_pk, 'pk_keys': pk_keys, 'Wq': Wq, 'keys_table': keys_table, 'values_table': values_table, 'Wo': Wo}
    _L0_ffn_all = _L0_ffn_setup()
    _L0_ffn_in = {k: v for k, v in _L0_ffn_all.items() if k in ('Wq_pk', 'pk_keys', 'Wq', 'keys_table', 'values_table', 'Wo')}
    del _L0_ffn_all
    return {'x': x, 'adj': adj, 'L0_gnn_e_weight': _L0_gnn_in['e_weight'], 'L0_gnn_Wx': _L0_gnn_in['Wx'], 'L0_gnn_Wh': _L0_gnn_in['Wh'], 'L0_gnn_b': _L0_gnn_in['b'], 'L0_ffn_Wq_pk': _L0_ffn_in['Wq_pk'], 'L0_ffn_pk_keys': _L0_ffn_in['pk_keys'], 'L0_ffn_Wq': _L0_ffn_in['Wq'], 'L0_ffn_keys_table': _L0_ffn_in['keys_table'], 'L0_ffn_values_table': _L0_ffn_in['values_table'], 'L0_ffn_Wo': _L0_ffn_in['Wo']}

def reference(x, adj, L0_gnn_e_weight, L0_gnn_Wx, L0_gnn_Wh, L0_gnn_b, L0_ffn_Wq_pk, L0_ffn_pk_keys, L0_ffn_Wq, L0_ffn_keys_table, L0_ffn_values_table, L0_ffn_Wo):
    import jax
    import jax.numpy as jnp

    def _L0_gnn_ref(seq_data, graph, e_weight, Wx, Wh, b):
        import jax, jax.numpy as jnp
        import numpy as np
        EPS = 1e-07
        beta = jnp.einsum('bld,du->blu', seq_data, e_weight)
        norm = jnp.maximum(jnp.sum(graph, axis=2), EPS)
        beta = beta / norm[:, :, None]
        agg = jnp.einsum('blu,blm->bmu', beta, graph)
        B, L, U = agg.shape
        h0 = jnp.zeros((B, U), dtype=agg.dtype)

        def step(h, x):
            h = jnp.tanh(x @ Wx + h @ Wh + b)
            return (h, h)
        _, ys = jax.lax.scan(step, h0, jnp.swapaxes(agg, 0, 1))
        return jnp.swapaxes(ys, 0, 1)

    def _L0_ffn_ref(x, Wq_pk, pk_keys, Wq, keys_table, values_table, Wo):
        import jax, jax.numpy as jnp
        import numpy as np
        DIM = 128
        HEADS = 8
        NUM_KEYS = 128
        NUM_KV = NUM_KEYS ** 2
        PK_TOPK = 16
        FINAL_TOPK = 16
        DIM_KEY = DIM // 2
        P = 2

        def _pk(x, Wq_pk, pk_keys):
            b, n, _ = x.shape
            q = (x @ Wq_pk).reshape(b, n, P, HEADS, DIM_KEY).transpose(2, 0, 1, 3, 4)
            sim = jnp.einsum('pbnhd,pkhd->pbnhk', q, pk_keys)
            scores, idx = jax.lax.top_k(sim, PK_TOPK)
            idx0 = idx[0]
            idx1 = idx[1] * NUM_KEYS
            index = (idx0[..., :, None] + idx1[..., None, :]).reshape(b, n, HEADS, PK_TOPK * PK_TOPK)
            score = (scores[0][..., :, None] + scores[1][..., None, :]).reshape(b, n, HEADS, PK_TOPK * PK_TOPK)
            final_scores, pk_idx = jax.lax.top_k(score, FINAL_TOPK)
            final_indices = jnp.take_along_axis(index, pk_idx, axis=-1)
            final_scores = jax.nn.softmax(final_scores, axis=-1)
            return (final_scores, final_indices)
        b, n, d = x.shape
        q = (x @ Wq).reshape(b, n, HEADS, DIM) * DIM ** (-0.5)
        kv_scores, indices = _pk(x, Wq_pk, pk_keys)
        offsets = jnp.arange(HEADS, dtype=indices.dtype) * NUM_KV
        ind = indices + offsets[None, None, :, None]
        k = jnp.einsum('bnhk,bnhkd->bnhd', kv_scores, keys_table[ind])
        v = jnp.einsum('bnhk,bnhkd->bnhd', kv_scores, values_table[ind])
        sim = jnp.einsum('bihd,bjhd->bhij', q, k)
        neg = -jnp.finfo(sim.dtype).max
        causal = jnp.tril(jnp.ones((n, n), dtype=bool))
        sim = jnp.where(causal, sim, neg)
        attn = jax.nn.softmax(sim, axis=-1)
        out = jnp.einsum('bhij,bjhd->bhid', attn, v)
        out = out.transpose(0, 2, 1, 3).reshape(b, n, HEADS * DIM)
        return out @ Wo
    x = x + _L0_gnn_ref(_layernorm(x, axis=-1), adj, L0_gnn_e_weight, L0_gnn_Wx, L0_gnn_Wh, L0_gnn_b)
    x = x + _L0_ffn_ref(_layernorm(x, axis=-1), L0_ffn_Wq_pk, L0_ffn_pk_keys, L0_ffn_Wq, L0_ffn_keys_table, L0_ffn_values_table, L0_ffn_Wo)
    return x

_drawn_inputs = setup_inputs


def setup_inputs(seed=0):
    import zlib

    import numpy as np

    out = dict(_drawn_inputs(seed))
    spreads = {'L0_gnn_b': (0.0, 0.1)}
    factors = {'L0_ffn_Wq_pk': 8.0,
     'L0_ffn_pk_keys': 8.0,
     'L0_ffn_Wq': 64.0,
     'L0_ffn_keys_table': 64.0,
     'L0_ffn_values_table': 8.0,
     'L0_ffn_Wo': 8.0}
    for name, (base, spread) in spreads.items():
        noise = np.random.default_rng([zlib.crc32(name.encode()), seed]).standard_normal(out[name].shape)
        drawn = base * np.exp(spread * noise) if base else spread * noise
        out[name] = jnp.asarray(drawn.astype(out[name].dtype))
    for name, factor in factors.items():
        out[name] = (out[name] * factor).astype(out[name].dtype)
    return out
```

```python
import concourse.bass as bass
from concourse import mybir
from contextlib import ExitStack


B, L, D = 32, 256, 128
H = 8
DK = D // 2
NK = 128
NKV = NK * NK
TOP = 16
C = L // 128
EPS_LN, EPS_NORM = 1e-5, 1e-7
LOWEST = -3.0e38
REPLACED = -3.4e38

PAIRS = [(0, 1, 16), (1, 1, 8), (2, 1, 5), (3, 1, 4), (4, 1, 3), (5, 3, 2), (8, 8, 1)]
NC = sum(ni * nj for _, ni, nj in PAIRS)
assert NC == sum(TOP // (i + 1) for i in range(TOP))

SLOTS = 4
CHUNKS = TOP // SLOTS
RING = 2 * CHUNKS
STEPS = 16
assert STEPS * B == 512


class Count:

    def __init__(self):
        self.value = 0

    def up(self):
        self.value += 1
        return self.value


def build(nc, x, adj, we, wx, wh, bias, wqpk, pkeys, wq, kv, wo, out):
    fp32, bf16, u32, i32 = mybir.dt.float32, mybir.dt.bfloat16, mybir.dt.uint32, mybir.dt.int32
    ALU = mybir.AluOpType
    ACT = mybir.ActivationFunctionType
    X = mybir.AxisListType.X

    ctx = ExitStack()
    with ctx:
        def sb(name, shape, dt=fp32):
            return ctx.enter_context(nc.sbuf_tensor(name, shape, dt))

        def sem(name):
            return ctx.enter_context(nc.semaphore(name))

        we_sb, wx_sb, wh_sb = (sb(n, [128, D]) for n in ("we_sb", "wx_sb", "wh_sb"))
        bias_sb = sb("bias_sb", [128, 1])
        wqpk_sb = sb("wqpk_sb", [128, 8, 128])
        keys_bd = sb("keys_bd", [128, 2, 4, 2, NK])
        wq_sb = sb("wq_sb", [128, H, D])
        wo_sb = sb("wo_sb", [128, H, D])
        ident = sb("ident", [128, 128])
        identb = sb("identb", [128, 128], bf16)
        maskb = sb("maskb", [128, 128], bf16)
        iota_i = sb("iota_i", [128, H * TOP], i32)
        iota_c = sb("iota_c", [128, NC])
        rowbase = sb("rowbase", [128, H, TOP])
        eps = sb("eps", [128, 1])

        x_all = sb("x_all", [128, B * C, D])
        h_all = sb("h_all", [128, L, B])
        xc_all = h_all[:, :, :].rearrange("p t b -> p (t b)").rearrange("p (r d) -> p r d", d=D)
        rows = sb("rows", [128, (L + STEPS) * B])
        G = rows[:, 0:RING * SLOTS * 2 * D].rearrange("p (s e) -> p s e", e=2 * D)
        agg_all = rows[:, :].rearrange("p (t b) -> p t b", b=B)
        diag = sb("diag", [128, 2, TOP, 128])
        sq = diag[:, :, :, :].rearrange("p a s n -> p a (s n)").rearrange("p a (r d) -> p a r d", d=D)
        KT = sb("KT", [128, H, L])
        V = sb("V", [128, H, C, D])
        adj_g = KT[:, :, :].rearrange("p (g r) m -> p g r m", g=2)
        v_flat = V[:, :, :, :].rearrange("p h c d -> p (h c) d")
        lnT_g = v_flat[:, 0:8, :].rearrange("p (g r) d -> p g r d", g=2)
        beta_g = v_flat[:, 8:16, :].rearrange("p (g r) d -> p g r d", g=2)
        sims = sb("sims", [128, 4, 2, 2, NK])
        xn_g = sims[:, 0:2, :, :, :].rearrange("p g a b k -> p g (a b) k")
        sums, mean, rstd = (sb(n, [128, B * C]) for n in ("sums", "mean", "rstd"))
        norm_g = sb("norm_g", [128, 2, 2 * C])
        rnorm_g = sb("rnorm_g", [128, 2, 2 * C])

        yT = sb("yT", [128, 128])
        x1 = sb("x1", [128, C, D])
        stats = sb("stats", [128, 6])
        mv = sb("mv", [128, 2])
        std = sb("std", [128, 1])
        rs = sb("rs", [128, 1])
        ln = sb("ln", [128, D])
        lnT = sb("lnT", [128, 128])
        qpkT = sb("qpkT", [128, 8, 128])
        qT = sb("qT", [128, C, H, 128])
        spare = sb("spare", [128, 4, NK])
        S1 = sb("S1", [128, 2, H, TOP])
        I1 = sb("I1", [128, 2, H, TOP], u32)
        I1f = sb("I1f", [128, 2, H, TOP])
        CV = sb("CV", [128, H, NC])
        CI = sb("CI", [128, H, NC])
        S2 = sb("S2", [128, H, TOP])
        P2 = sb("P2", [128, H, TOP], u32)
        P2f = sb("P2f", [128, H, TOP])
        hot = sb("hot", [128, 2, TOP, NC])
        h_ring = hot[:, :, :, :].rearrange("p a k n -> p (a k n)")[:, 0:2 * STEPS * B] \
            .rearrange("p (s b) -> p s b", b=B)
        rowf = sb("rowf", [128, H, TOP])
        idx = sb("idx", [128, C, H * TOP], u32)
        wexp = sb("wexp", [128, H, TOP])
        wsum = sb("wsum", [128, H])
        w = sb("w", [128, C, H, TOP])
        nmax = sb("nmax", [128, 2])
        rsum = sb("rsum", [128, 2])
        rrec = sb("rrec", [128, 2])
        P = sb("P", [128, 2, L])
        PT = sb("PT", [128, C, 128])
        oT = sb("oT", [128, 128])
        y = sb("y", [128, C, D])

        bank = [ctx.enter_context(nc.psum_tensor(f"bank{i}", [128, 512], fp32)) for i in range(8)]
        kT_ps, v_ps, score_ps, pT_ps, wo_ps = bank[0:5]
        o_ps = pT_ps[:, 256:512]
        ident_ps = bank[5][:, 0:128]
        fill = bank[6:8]

        const_landed = sem("const_landed")
        x_landed = [sem(f"x_landed{q}") for q in range(4)]
        adj_landed = [sem(f"adj_landed{g}") for g in range(2)]
        consts = sem("consts")
        setup = sem("setup")
        v_chain = sem("v_chain")
        centered = sem("centered")
        squared = sem("squared")
        vars_ready = sem("vars_ready")
        std_all = sem("std_all")
        adj_free = sem("adj_free")
        xn_ready = sem("xn_ready")
        norm_ready = sem("norm_ready")
        xnT_done = sem("xnT_done")
        lnTg_ready = sem("lnTg_ready")
        beta_done = sem("beta_done")
        betag_ready = sem("betag_ready")
        agg_done = sem("agg_done")
        agg_ready = sem("agg_ready")
        h_ready = sem("h_ready")
        z_done = sem("z_done")
        h_copied = sem("h_copied")

        landed = [sem(f"landed{s}") for s in range(RING)]
        gate = sem("gate")
        ws_done = sem("ws_done")
        diag_ready = sem("diag_ready")
        idx_ready = sem("idx_ready")
        kv_ready = sem("kv_ready")
        scores_done = sem("scores_done")
        max_ready = sem("max_ready")
        exp_ready = sem("exp_ready")
        p_ready = sem("p_ready")
        pT_done = sem("pT_done")
        pT_ready = sem("pT_ready")
        o_done = sem("o_done")
        oT_ready = sem("oT_ready")
        wo_done = sem("wo_done")
        y_ready = sem("y_ready")
        stored = [sem(f"stored{c}") for c in range(C)]
        yT_ready = sem("yT_ready")
        yback_done = sem("yback_done")
        mv_ready = sem("mv_ready")
        std_ready = sem("std_ready")
        ln_ready = sem("ln_ready")
        lnT_done = sem("lnT_done")
        lnT_ready = sem("lnT_ready")
        fill_done = sem("fill_done")
        fill_ready = sem("fill_ready")
        pad_ready = sem("pad_ready")
        gaps = sem("gaps")
        gexp = sem("gexp")

        N_CONST = 11
        NG = B // 2
        block = ctx.enter_context(nc.Block())

        @block.sync
        def _(sp):
            for q in range(4):
                sp.dma_start(x_all[:, 16 * q:16 * q + 16, :],
                             x[8 * q:8 * q + 8].rearrange("b (c p) d -> p (b c) d", p=128)).then_inc(x_landed[q], 16)
            sp.sem_inc(adj_free, 2)
            with sp.Fori(0, NG // 2) as i:
                for g in range(2):
                    sp.wait_ge(adj_free, i * 2 + (g + 1))
                    for k in range(2):
                        sp.dma_start(adj_g[:, g, 2 * k:2 * k + 2, :],
                                     adj[bass.ds(i * 4 + (2 * g + k), 1)]
                                     .rearrange("b (c p) m -> p (b c) m", p=128)).then_inc(adj_landed[g], 16)

            def store(n, c):
                sp.wait_ge(y_ready, n * 2 + (c + 2))
                sp.dma_start(out[bass.ds(n, 1), 128 * c:128 * c + 128, :].rearrange("b p d -> p (b d)"),
                             y[:, c, :]).then_inc(stored[c], 16)

            with sp.Fori(0, B) as n:
                for c in range(C):
                    store(n, c)
            for c in range(C):
                sp.wait_ge(stored[c], 16 * (B + 1))

        @block.gpsimd
        def _(pool):
            pool.memset(ident[:, :], 0.0).then_inc(consts, 1)
            pool.memset(identb[:, :], 0.0).then_inc(consts, 1)
            pool.memset(maskb[:, :], 0.0).then_inc(consts, 1)
            pool.memset(h_ring[:, 2 * STEPS - 1, :], 0.0).then_inc(consts, 1)
            pool.memset(eps[:, :], EPS_LN).then_inc(consts, 1)
            pool.iota(iota_i[:, :], pattern=[[NKV, H], [0, TOP]], base=0, channel_multiplier=0).then_inc(consts, 1)
            pool.wait_ge(consts, 3)
            for m in (ident, identb):
                pool.affine_select(out=m[:, :], in_=m[:, :], compare_op=ALU.not_equal, fill=1.0,
                                   base=0, pattern=[[-1, 128]], channel_multiplier=1).then_inc(consts, 1)
            pool.affine_select(out=maskb[:, :], in_=maskb[:, :], compare_op=ALU.is_ge, fill=LOWEST,
                               base=0, pattern=[[-1, 128]], channel_multiplier=1).then_inc(consts, 1)
            pool.wait_ge(setup, 1)
            pool.iota(iota_i[:, 0:NC], pattern=[[1, NC]], base=0, channel_multiplier=0).then_inc(consts, 1)

            def gather(n, c):
                pool.wait_ge(idx_ready, n * 2 + (c + 1))
                pool.sem_inc(gate, 1)
                for h in range(H):
                    for k in range(CHUNKS):
                        slot = (h % 2) * CHUNKS + k
                        pool.wait_ge(ws_done, n * (C * H * CHUNKS) + ((c * H + h) * CHUNKS + k + 1))
                        pool.sem_inc(gate, 1)
                        for s in range(SLOTS):
                            col = h * TOP + k * SLOTS + s
                            pool.indirect_dma_start(
                                G[:, slot * SLOTS + s, :], None, kv,
                                bass.IndirectOffsetOnAxis(idx[:, c, col:col + 1], 0)).then_inc(landed[slot], 16)

            with pool.Fori(0, B) as n:
                for c in range(C):
                    gather(n, c)

        @block.scalar
        def _(act):
            for dst, src in ((we_sb[:, :], we), (wx_sb[:, :], wx), (wh_sb[:, :], wh),
                             (bias_sb[:, :], bias.rearrange("(p a) -> p a", a=1)),
                             (wqpk_sb[:, :, :].rearrange("p a b -> p (a b)"), wqpk),
                             (wq_sb[:, :, :].rearrange("p a b -> p (a b)"), wq),
                             (wo_sb[:, :, :], wo.rearrange("(h p) d -> p h d", p=128))):
                act.dma_start(dst, src).then_inc(const_landed, 16)
            act.wait_ge(setup, 3)
            for half in range(2):
                for hh in range(2):
                    act.dma_start(keys_bd[DK * hh:DK * hh + DK, half, :, hh, :],
                                  pkeys[DK * hh:DK * hh + DK, half]).then_inc(const_landed, 16)
            act.wait_ge(consts, 9)
            nc.scalar.activation(ident_ps, ident[:, :], ACT.Copy).then_inc(setup, 1)

            for q in range(4):
                act.wait_ge(centered, q + 1)
                nc.scalar.activation(sq[:, q % 2], xc_all[:, 16 * q:16 * q + 16, :], ACT.Square).then_inc(squared, 1)
            act.wait_ge(vars_ready, 4)
            nc.scalar.activation(mean[:, :], sums[:, :], ACT.Sqrt, bias=eps[:, :], scale=1.0 / D).then_inc(std_all, 1)

            with act.Fori(0, NG // 2) as i:
                for g in range(2):
                    act.wait_ge(xnT_done, i * 2 + (g + 1))
                    nc.scalar.activation(lnT_g[:, g].rearrange("p r d -> p (r d)"), bank[0][:, :],
                                         ACT.Copy).then_inc(lnTg_ready, 1)
                    act.wait_ge(norm_ready, i * 2 + (g + 1))
                    act.sem_inc(gate, 1)
                    act.wait_ge(beta_done, i * 2 + (g + 1))
                    for r in range(2 * C):
                        nc.scalar.activation(beta_g[:, g, r, :], bank[1][:, 128 * r:128 * r + 128],
                                             ACT.Copy, scale=rnorm_g[:, g, r:r + 1]).then_inc(betag_ready, 1)

            act.sem_inc(h_copied, 2)
            with act.Fori(0, L // STEPS // 2) as i:
                for k in range(2):
                    act.wait_ge(h_copied, i * 2 + (k + 1))
                    act.sem_inc(gate, 1)
                    for s in range(STEPS):
                        act.wait_ge(z_done, i * (2 * STEPS) + (k * STEPS + s + 1))
                        nc.scalar.activation(h_ring[:, k * STEPS + s, :], bank[k][:, B * s:B * s + B],
                                             ACT.Tanh, bias=bias_sb[:, :]).then_inc(h_ready, 1)

            def evac_kv(n, c, h):
                u = C * H
                for k, (dst, src) in enumerate(((KT[:, h, 128 * c:128 * c + 128], kT_ps[:, 0:128]),
                                                (V[:, h, c, :], v_ps[:, 0:128]))):
                    if k == 0:
                        act.wait_ge(ws_done, n * (u * CHUNKS) + ((c * H + h + 1) * CHUNKS + RING))
                    nc.scalar.activation(dst, src, ACT.Copy).then_inc(kv_ready, 1)

            def evac_attention(n, c, h):
                j = c * H + h
                act.wait_ge(pT_done, n * (C * H) + (j + 1))
                nc.scalar.activation(PT[:, 0:c + 1, :], pT_ps[:, 0:128 * (c + 1)].rearrange("p (a i) -> p a i", i=128),
                                     ACT.Copy).then_inc(pT_ready, 1)
                act.wait_ge(o_done, n * (C * H) + (j + 1))
                nc.scalar.activation(oT[:, :], o_ps[:, 0:128], ACT.Copy).then_inc(oT_ready, 1)

            def exponential(n, c, h):
                act.wait_ge(max_ready, n * (C * H) + (c * H + h + 1))
                nc.scalar.activation(P[:, h % 2, 0:128 * (c + 1)], score_ps[:, 0:128 * (c + 1)], ACT.Exp,
                                     bias=nmax[:, h % 2:h % 2 + 1],
                                     accum_out=rsum[:, h % 2:h % 2 + 1]).then_inc(exp_ready, 1)

            def evac_fill(n, c, f, dst, scale=1.0):
                act.wait_ge(fill_done, n * (8 * C) + (8 * c + f + 1))
                nc.scalar.activation(dst, fill[f % 2][:, :], ACT.Copy, scale=scale).then_inc(fill_ready, 1)

            def route(n, c, step):
                if step == 0:
                    act.wait_ge(mv_ready, n * 2 + (c + 1))
                    nc.scalar.activation(std[:, :], mv[:, 1:2], ACT.Sqrt, bias=eps[:, :]).then_inc(std_ready, 1)
                    act.wait_ge(lnT_done, n * 2 + (c + 1))
                    nc.scalar.activation(lnT[:, :], fill[1][:, 128:256], ACT.Copy).then_inc(lnT_ready, 1)
                    for f in range(2):
                        evac_fill(n, c, f, qpkT[:, 4 * f:4 * f + 4, :].rearrange("p a t -> p (a t)"))
                    for f in range(2):
                        evac_fill(n, c, 2 + f, qT[:, c, 4 * f:4 * f + 4, :].rearrange("p a t -> p (a t)"),
                                  float(D) ** -0.5)
                if step in (1, 2):
                    for hp in (2 * step - 2, 2 * step - 1):
                        evac_fill(n, c, 4 + hp, sims[:, hp].rearrange("p a b k -> p (a b k)"))
                if step == 5:
                    act.wait_ge(gaps, n * 2 + (c + 1))
                    nc.scalar.activation(wexp[:, :, :], wexp[:, :, :], ACT.Exp).then_inc(gexp, 1)

            def tile(n, c, nxt):
                for h in range(H):
                    evac_kv(n, c, h)
                    if h:
                        evac_attention(n, c, h - 1)
                    exponential(n, c, h)
                    if nxt is not None:
                        route(*nxt, h)
                evac_attention(n, c, H - 1)

            for step in range(H):
                route(0, 0, step)
            with act.Fori(0, B - 1) as n:
                tile(n, 0, (n, 1))
                tile(n, 1, (n + 1, 0))
            tile(B - 1, 0, (B - 1, 1))
            tile(B - 1, 1, None)

        @block.tensor
        def _(pe):
            pe.wait_ge(const_landed, 16 * N_CONST)
            pe.wait_ge(consts, 10)
            pe.wait_ge(setup, 4)
            with pe.Fori(0, NG // 2) as i:
                for g in range(2):
                    pe.wait_ge(xn_ready, i * 2 + (g + 1))
                    for r in range(2 * C):
                        last = nc.tensor.transpose(bank[0][:, 128 * r:128 * r + 128], xn_g[:, g, r, :], ident[:, :])
                    last.then_inc(xnT_done, 1)
                    pe.wait_ge(lnTg_ready, i * 2 + (g + 1))
                    for r in range(2 * C):
                        last = nc.tensor.matmul(bank[1][:, 128 * r:128 * r + 128], lnT_g[:, g, r, :], we_sb[:, :],
                                                start=True, stop=True)
                    last.then_inc(beta_done, 1)
                    pe.wait_ge(agg_ready, i * 2 + (g + 1))
                    pe.sem_inc(gate, 1)
                    pe.wait_ge(betag_ready, i * (4 * C) + (2 * C * (g + 1)))
                    for k in range(2):
                        for c in range(C):
                            last = nc.tensor.matmul(bank[2 + g][:, L * k:L * k + L], beta_g[:, g, C * k + c, :],
                                                    adj_g[:, g, C * k + c, :], start=(c == 0), stop=(c == C - 1))
                    last.then_inc(agg_done, 1)

            pe.wait_ge(agg_ready, NG + 2)
            pe.wait_ge(pad_ready, 1)
            nc.tensor.matmul(bank[0][:, :], wx_sb[:, :], agg_all[:, 0:STEPS, :].rearrange("p t b -> p (t b)"),
                             start=True, stop=True)
            pe.sem_inc(h_ready, 1)
            with pe.Fori(0, L // STEPS // 2) as i:
                for k in range(2):
                    for s in range(STEPS):
                        pe.wait_ge(h_ready, i * (2 * STEPS) + (k * STEPS + s + 1))
                        nc.tensor.matmul(bank[k][:, B * s:B * s + B], wh_sb[:, :],
                                         h_ring[:, (k * STEPS + s - 1) % (2 * STEPS), :],
                                         start=False, stop=True,
                                         skip_group_check=True).then_inc(z_done, 1)
                        if s == 1:
                            t0 = bass.ds((i * (2 * STEPS) + (k + 1) * STEPS) * B, STEPS * B)
                            nc.tensor.matmul(bank[1 - k][:, :], wx_sb[:, :], rows[:, t0], start=True, stop=True)

            pe.sem_inc(ws_done, RING)
            pe.sem_inc(kv_ready, 2)
            pe.sem_inc(exp_ready, 1)
            pe.sem_inc(y_ready, 1)
            pe.sem_inc(fill_ready, 2)

            def weighted_sums(n, c, h):
                j = c * H + h
                pe.wait_ge(diag_ready, n * (C * H) + (j + 1))
                pe.sem_inc(gate, 1)
                pe.wait_ge(kv_ready, n * (2 * C * H) + (2 * j + 2))
                pe.sem_inc(gate, 1)
                for k in range(CHUNKS):
                    slot = (h % 2) * CHUNKS + k
                    pe.wait_ge(landed[slot], n * (C * H // 2 * SLOTS * 16) + (j // 2 + 1) * SLOTS * 16)
                    for s in range(k * SLOTS, k * SLOTS + SLOTS):
                        at = (h % 2) * TOP + s
                        ends = dict(start=(s == 0), stop=(s == TOP - 1))
                        nc.tensor.matmul(kT_ps[:, 0:128], G[:, at, 0:D], diag[:, h % 2, s, :], **ends)
                        last = nc.tensor.matmul(v_ps[:, 0:128], diag[:, h % 2, s, :], G[:, at, D:2 * D], **ends)
                    last.then_inc(ws_done, 1)

            def scores(n, c, h):
                j = c * H + h
                pe.wait_ge(exp_ready, n * (C * H) + (j + 1))
                own = score_ps[:, 128 * c:128 * c + 128]
                nc.tensor.matmul(own, identb[:, :], maskb[:, :], start=True, stop=False)
                pe.wait_ge(kv_ready, n * (2 * C * H) + (2 * j + 4))
                last = nc.tensor.matmul(own, qT[:, c, h, :], KT[:, h, 128 * c:128 * c + 128], start=False, stop=True)
                if c:
                    last = nc.tensor.matmul(score_ps[:, 0:128], qT[:, c, h, :], KT[:, h, 0:128], start=True, stop=True)
                last.then_inc(scores_done, 1)

            def attention(n, c, h):
                j = c * H + h
                pe.wait_ge(p_ready, n * (C * H) + (j + 1))
                for a in range(c + 1):
                    last = nc.tensor.transpose(pT_ps[:, 128 * a:128 * a + 128], P[:, h % 2, 128 * a:128 * a + 128],
                                               ident[:, :])
                last.then_inc(pT_done, 1)
                pe.wait_ge(pT_ready, n * (C * H) + (j + 1))
                for a in range(c + 1):
                    last = nc.tensor.matmul(o_ps[:, 0:128], V[:, h, a, :], PT[:, a, :], start=(a == 0), stop=(a == c))
                last.then_inc(o_done, 1)
                if h == 0:
                    pe.wait_ge(y_ready, n * 2 + (c + 1))
                    pe.sem_inc(gate, 1)
                pe.wait_ge(oT_ready, n * (C * H) + (j + 1))
                last = nc.tensor.matmul(wo_ps[:, 0:128], oT[:, :], wo_sb[:, h, :], start=(h == 0), stop=(h == H - 1))
                if h == H - 1:
                    last.then_inc(wo_done, 1)

            def fill_bank(n, c, f, products):
                pe.wait_ge(fill_ready, n * (8 * C) + (8 * c + f + 1))
                for at, lhsT, rhs in products:
                    last = nc.tensor.matmul(fill[f % 2][:, at], lhsT, rhs, start=True, stop=True)
                last.then_inc(fill_done, 1)

            def route(n, c, step):
                if step == 0:
                    pe.wait_ge(fill_ready, n * (8 * C) + (8 * c + 2))
                    pe.sem_inc(gate, 1)
                    pe.wait_ge(yT_ready, n * 2 + (c + 1))
                    nc.tensor.transpose(fill[1][:, 0:128], yT[:, :], ident[:, :]).then_inc(yback_done, 1)
                    pe.wait_ge(ln_ready, n * 2 + (c + 1))
                    nc.tensor.transpose(fill[1][:, 128:256], ln[:, :], ident[:, :]).then_inc(lnT_done, 1)
                    pe.wait_ge(lnT_ready, n * 2 + (c + 1))
                    for f in range(2):
                        fill_bank(n, c, f, [(slice(128 * a, 128 * a + 128), wqpk_sb[:, 4 * f + a, :], lnT[:, :])
                                            for a in range(4)])
                    for f in range(2):
                        fill_bank(n, c, 2 + f, [(slice(128 * a, 128 * a + 128), wq_sb[:, 4 * f + a, :], lnT[:, :])
                                                for a in range(4)])
                if step in (1, 2):
                    for hp in (2 * step - 2, 2 * step - 1):
                        fill_bank(n, c, 4 + hp, [(slice(256 * half, 256 * half + 256), qpkT[:, 4 * half + hp, :],
                                                  keys_bd[:, half, hp, :, :].rearrange("p a k -> p (a k)"))
                                                 for half in range(2)])

            def tile(n, c, nxt):
                for h in range(H):
                    weighted_sums(n, c, h)
                    scores(n, c, h)
                    if h:
                        attention(n, c, h - 1)
                    if nxt is not None:
                        route(*nxt, h)
                attention(n, c, H - 1)

            for step in range(H):
                route(0, 0, step)
            with pe.Fori(0, B - 1) as n:
                tile(n, 0, (n, 1))
                tile(n, 1, (n + 1, 0))
            tile(B - 1, 0, (B - 1, 1))
            tile(B - 1, 1, None)

        @block.vector
        def _(dve):
            chain = Count()

            def follow():
                dve.wait_ge(v_chain, chain.value)

            def clear_chain():
                follow()
                dve.sem_clear(v_chain)
                chain.value = 0

            dve.wait_ge(consts, 6)
            nc.vector.tensor_copy(rowbase[:, :, :].rearrange("p h k -> p (h k)"), iota_i[:, :]).then_inc(setup, 1)
            nc.vector.memset(agg_all[:, L:L + STEPS, :], 0.0).then_inc(pad_ready, 1)
            nc.vector.memset(keys_bd[:, 0, :, :, :], 0.0).then_inc(setup, 1)
            nc.vector.memset(keys_bd[:, 1, :, :, :], 0.0).then_inc(setup, 1)
            dve.wait_ge(consts, 10)
            nc.vector.tensor_copy(iota_c[:, :], iota_i[:, 0:NC]).then_inc(v_chain, 1)
            chain.up()

            def variance(q):
                dve.wait_ge(squared, q + 1)
                nc.vector.reduce_sum(sums[:, 16 * q:16 * q + 16], sq[:, q % 2], axis=X).then_inc(vars_ready, 1)

            for q in range(4):
                part = slice(16 * q, 16 * q + 16)
                dve.wait_ge(x_landed[q], 16)
                nc.vector.reduce_sum(mean[:, part], x_all[:, part, :], axis=X).then_inc(v_chain, 1)
                chain.up()
                follow()
                nc.vector.tensor_scalar(mean[:, part], mean[:, part], 1.0 / D, None, ALU.mult).then_inc(v_chain, 1)
                chain.up()
                follow()
                nc.vector.tensor_tensor(xc_all[:, part, :], x_all[:, part, :],
                                        mean[:, part].unsqueeze(2).broadcast_to([128, 16, D]),
                                        ALU.subtract).then_inc(centered, 1)
                if q:
                    variance(q - 1)
            variance(3)
            dve.wait_ge(std_all, 1)
            nc.vector.reciprocal(rstd[:, :], mean[:, :]).then_inc(v_chain, 1)
            chain.up()
            clear_chain()

            dve.sem_inc(agg_ready, 2)

            with dve.Fori(0, NG // 2) as i:
                for g in range(2):
                    nc.vector.tensor_tensor(xn_g[:, g, :, :], xc_all[:, bass.ds(i * 8 + 4 * g, 4), :],
                                            rstd[:, bass.ds(i * 8 + 4 * g, 4)].unsqueeze(2).broadcast_to([128, 4, D]),
                                            ALU.mult).then_inc(xn_ready, 1)
                    dve.wait_ge(adj_landed[g], i * 32 + 32)
                    nc.vector.reduce_sum(norm_g[:, g, :], adj_g[:, g, :, :], axis=X).then_inc(v_chain, 1)
                    chain.up()
                    follow()
                    nc.vector.tensor_scalar(norm_g[:, g, :], norm_g[:, g, :], EPS_NORM, None,
                                            ALU.max).then_inc(v_chain, 1)
                    chain.up()
                    follow()
                    nc.vector.reciprocal(rnorm_g[:, g, :], norm_g[:, g, :]).then_inc(norm_ready, 1)
                    for k in ((), (0, 1))[g]:
                        dve.wait_ge(agg_done, i * 2 + (k + 1))
                        dve.sem_inc(gate, 1)
                        nc.vector.tensor_copy(
                            agg_all[:, 0:L, bass.ds(i * 4 + 2 * k, 2)].rearrange("p t b -> p b t"),
                            bank[2 + k][:, :].rearrange("p (b t) -> p b t", b=2)).then_inc(agg_ready, 1)
                        dve.sem_inc(adj_free, 1)
                clear_chain()

            with dve.Fori(0, L // STEPS // 2) as i:
                for k in range(2):
                    dve.wait_ge(h_ready, i * (2 * STEPS) + (k + 1) * STEPS + 1)
                    dve.sem_inc(gate, 1)
                    nc.vector.tensor_copy(
                        h_all[:, bass.ds(i * (2 * STEPS) + k * STEPS, STEPS), :],
                        h_ring[:, k * STEPS:k * STEPS + STEPS, :]).then_inc(h_copied, 1)
            dve.wait_ge(h_copied, L // STEPS + 2)
            for c in range(C):
                dve.sem_inc(stored[c], 16)

            def diagonal(n, c, h):
                dve.wait_ge(ws_done, n * (C * H * CHUNKS) + ((c * H + h - 1) * CHUNKS + RING))
                dve.sem_inc(gate, 1)
                nc.vector.tensor_tensor(diag[:, h % 2, :, :],
                                        ident_ps.unsqueeze(1).broadcast_to([128, TOP, 128]),
                                        w[:, c, h, :].unsqueeze(2).broadcast_to([128, TOP, 128]),
                                        ALU.mult).then_inc(diag_ready, 1)

            def row_max(n, c, h):
                dve.wait_ge(scores_done, n * (C * H) + (c * H + h + 1))
                nc.vector.tensor_reduce(nmax[:, h % 2:h % 2 + 1], score_ps[:, 0:128 * (c + 1)], axis=X, op=ALU.max,
                                        negate=True).then_inc(max_ready, 1)

            def normalise(n, c, h):
                dve.wait_ge(exp_ready, n * (C * H) + (c * H + h + 2))
                nc.vector.reciprocal(rrec[:, h % 2:h % 2 + 1], rsum[:, h % 2:h % 2 + 1]).then_inc(v_chain, 1)
                chain.up()
                follow()
                nc.vector.tensor_scalar(P[:, h % 2, 0:128 * (c + 1)], P[:, h % 2, 0:128 * (c + 1)],
                                        rrec[:, h % 2:h % 2 + 1], None, ALU.mult).then_inc(p_ready, 1)

            def top16(jobs):
                marks = []
                for src, _, best, _ in jobs:
                    nc.vector.max(best[:, 0:8], src).then_inc(v_chain, 1)
                    marks.append(chain.up())
                for j, (src, rest, best, at) in enumerate(jobs):
                    dve.wait_ge(v_chain, marks[j])
                    nc.vector.match_replace(rest, best[:, 0:8], src, REPLACED).then_inc(v_chain, 1)
                    marks[j] = chain.up()
                    nc.vector.max_index(at[:, 0:8], best[:, 0:8], src).then_inc(v_chain, 1)
                    chain.up()
                for j, (_, rest, best, _) in enumerate(jobs):
                    dve.wait_ge(v_chain, marks[j])
                    nc.vector.max(best[:, 8:16], rest).then_inc(v_chain, 1)
                    marks[j] = chain.up()
                for j, (_, rest, best, at) in enumerate(jobs):
                    dve.wait_ge(v_chain, marks[j])
                    nc.vector.max_index(at[:, 8:16], best[:, 8:16], rest).then_inc(v_chain, 1)
                    chain.up()

            def layernorm(n, c):
                nc.vector.tensor_copy(yT[:, :], h_all[:, 128 * c:128 * c + 128, bass.ds(n, 1)]
                                      .rearrange("p t b -> p (t b)")).then_inc(yT_ready, 1)
                dve.wait_ge(yback_done, n * 2 + (c + 1))
                dve.sem_inc(gate, 1)
                nc.vector.tensor_tensor(x1[:, c, :], x_all[:, bass.ds(n * 2 + c, 1), :].rearrange("p r d -> p (r d)"),
                                        fill[1][:, 0:128], ALU.add).then_inc(v_chain, 1)
                chain.up()
                follow()
                nc.vector.bn_stats(stats[:, :], x1[:, c, :]).then_inc(v_chain, 1)
                chain.up()
                follow()
                nc.vector.bn_aggr(mv[:, :], stats[:, :]).then_inc(mv_ready, 1)
                dve.wait_ge(std_ready, n * 2 + (c + 1))
                nc.vector.reciprocal(rs[:, :], std[:, :]).then_inc(v_chain, 1)
                chain.up()
                follow()
                nc.vector.tensor_scalar(ln[:, :], x1[:, c, :], mv[:, 0:1], rs[:, :],
                                        ALU.subtract, ALU.mult).then_inc(ln_ready, 1)

            def half_keys(n, c, step):
                for hp in (2 * step - 2, 2 * step - 1):
                    dve.wait_ge(fill_ready, n * (8 * C) + (8 * c + 4 + hp + 3))
                    dve.sem_inc(gate, 1)
                    top16([(sims[:, hp, half, hh, :], spare[:, 2 * half + hh, :], S1[:, half, 2 * hp + hh, :],
                            I1[:, half, 2 * hp + hh, :]) for half in range(2) for hh in range(2)])

            def pairs(n, c):
                follow()
                nc.vector.tensor_tensor(I1f[:, 0], I1[:, 0], rowbase[:, :, :], ALU.add).then_inc(v_chain, 1)
                chain.up()
                nc.vector.tensor_scalar(I1f[:, 1], I1[:, 1], float(NK), None, ALU.mult).then_inc(v_chain, 1)
                chain.up()
                for dst, src in ((CV, S1), (CI, I1f)):
                    at = 0
                    if src is I1f:
                        follow()
                    for i0, ni, nj in PAIRS:
                        if ni == 1:
                            shape = [128, H, nj]
                            o = dst[:, :, at:at + nj]
                            a, b = src[:, 0, :, i0:i0 + 1].broadcast_to(shape), src[:, 1, :, 0:nj]
                        elif nj == 1:
                            shape = [128, H, ni]
                            o = dst[:, :, at:at + ni]
                            a, b = src[:, 0, :, i0:i0 + ni], src[:, 1, :, 0:1].broadcast_to(shape)
                        else:
                            shape = [128, H, ni, nj]
                            o = dst[:, :, at:at + ni * nj].rearrange("p h (i j) -> p h i j", j=nj)
                            a = src[:, 0, :, i0:i0 + ni].unsqueeze(3).broadcast_to(shape)
                            b = src[:, 1, :, 0:nj].unsqueeze(2).broadcast_to(shape)
                        nc.vector.tensor_tensor(o, a, b, ALU.add).then_inc(v_chain, 1)
                        chain.up()
                        at += ni * nj
                follow()
                for h0 in (0, 4):
                    top16([(CV[:, h, :], spare[:, h - h0, 0:NC], S2[:, h, :], P2[:, h, :])
                           for h in range(h0, h0 + 4)])
                follow()
                nc.vector.tensor_copy(P2f[:, :, :], P2[:, :, :]).then_inc(v_chain, 1)
                chain.up()
                nc.vector.tensor_tensor(wexp[:, :, :], S2[:, :, :], S2[:, :, 0:1].broadcast_to([128, H, TOP]),
                                        ALU.subtract).then_inc(gaps, 1)

            def table_rows(h0):
                hs = slice(h0, h0 + 2)
                shape = [128, 2, TOP, NC]
                follow()
                nc.vector.tensor_tensor(
                    hot[:, :, :, :], P2f[:, hs, :].unsqueeze(3).broadcast_to(shape),
                    iota_c[:, :].unsqueeze(1).unsqueeze(1).broadcast_to(shape), ALU.is_equal).then_inc(v_chain, 1)
                chain.up()
                follow()
                nc.vector.tensor_tensor(hot[:, :, :, :], hot[:, :, :, :],
                                        CI[:, hs, :].unsqueeze(2).broadcast_to(shape), ALU.mult).then_inc(v_chain, 1)
                chain.up()
                follow()
                nc.vector.reduce_sum(rowf[:, hs, :], hot[:, :, :, :], axis=X).then_inc(v_chain, 1)
                chain.up()

            def weights(n, c):
                dve.wait_ge(gexp, n * 2 + (c + 1))
                nc.vector.reduce_sum(wsum[:, :], wexp[:, :, :], axis=X).then_inc(v_chain, 1)
                chain.up()
                follow()
                nc.vector.reciprocal(wsum[:, :], wsum[:, :]).then_inc(v_chain, 1)
                chain.up()
                follow()
                nc.vector.tensor_tensor(w[:, c, :, :], wexp[:, :, :],
                                        wsum[:, :].unsqueeze(2).broadcast_to([128, H, TOP]),
                                        ALU.mult).then_inc(v_chain, 1)
                chain.up()
                nc.vector.tensor_copy(idx[:, c, :], rowf[:, :, :].rearrange("p h k -> p (h k)")).then_inc(idx_ready, 1)

            def route(n, c, step):
                if step == 0:
                    layernorm(n, c)
                if step in (1, 2):
                    half_keys(n, c, step)
                if step == 3:
                    pairs(n, c)
                if step == 4:
                    table_rows(0)
                    table_rows(2)
                if step == 5:
                    table_rows(4)
                    table_rows(6)
                    weights(n, c)

            def tile(n, c, nxt):
                for h in range(H):
                    if h:
                        normalise(n, c, h - 1)
                    if h < H - 1:
                        diagonal(n, c, h + 1)
                    elif nxt is not None:
                        follow()
                        if c == 0:
                            diagonal(n, 1, 0)
                        else:
                            diagonal(n + 1, 0, 0)
                    row_max(n, c, h)
                    if nxt is not None:
                        route(*nxt, h)
                normalise(n, c, H - 1)
                dve.wait_ge(stored[c], n * 16 + 16)
                dve.sem_inc(gate, 1)
                dve.wait_ge(wo_done, n * 2 + (c + 1))
                nc.vector.tensor_tensor(y[:, c, :], x1[:, c, :], wo_ps[:, 0:128], ALU.add).then_inc(y_ready, 1)
                clear_chain()

            for step in range(H):
                route(0, 0, step)
            clear_chain()
            dve.wait_ge(setup, 4)
            diagonal(0, 0, 0)
            with dve.Fori(0, B - 1) as n:
                tile(n, 0, (n, 1))
                tile(n, 1, (n + 1, 0))
            tile(B - 1, 0, (B - 1, 1))
            tile(B - 1, 1, None)


_ORDER = ["x", "adj", "L0_gnn_e_weight", "L0_gnn_Wx", "L0_gnn_Wh", "L0_gnn_b", "L0_ffn_Wq_pk",
          "pk_keys_t", "L0_ffn_Wq", "key_value_rows", "L0_ffn_Wo"]


def kernel(**inputs):
    import numpy as _np
    import concourse.bacc as _bacc
    from concourse import mybir as _mybir
    from concourse.bass_utils import run_bass_kernel_spmd as _run

    arrays = {k: _np.asarray(v) for k, v in inputs.items()}
    keys = arrays.pop("L0_ffn_pk_keys").transpose(2, 3, 0, 1).reshape(H // 2, 2 * DK, 2, NK)
    arrays["pk_keys_t"] = _np.ascontiguousarray(keys.transpose(1, 2, 0, 3))
    arrays["key_value_rows"] = _np.concatenate(
        [arrays.pop("L0_ffn_keys_table"), arrays.pop("L0_ffn_values_table")], axis=1)

    nc = _bacc.Bacc("TRN2", target_bir_lowering=False, num_devices=1)
    feeds, args = {}, []
    for name in _ORDER:
        a = _np.ascontiguousarray(arrays[name])
        feeds[f"in_{name}"] = a
        args.append(nc.dram_tensor(f"in_{name}", a.shape, _mybir.dt.from_np(a.dtype), kind="ExternalInput").ap())
    args.append(nc.dram_tensor("out_x", (B, L, D), _mybir.dt.float32, kind="ExternalOutput").ap())
    build(nc, *args)
    return _run(nc, [feeds], core_ids=[0]).results[0]["out_x"]
```

```python
import concourse.bass as bass
from concourse import mybir
from contextlib import ExitStack
import itertools


B, L, D = 32, 256, 128
H = 8
DK = D // 2
NK = 128
NKV = NK * NK
TOP = 16
C = L // 128
EPS_LN, EPS_NORM = 1e-5, 1e-7
LOWEST = -3.0e38
REPLACED = -3.4e38

PAIRS = [(0, 1, 16), (1, 1, 8), (2, 1, 5), (3, 1, 4), (4, 1, 3), (5, 3, 2), (8, 8, 1)]
NC = sum(ni * nj for _, ni, nj in PAIRS)
assert NC == sum(TOP // (i + 1) for i in range(TOP))

SLOTS = 4
CHUNKS = TOP // SLOTS
RING = 2 * CHUNKS
STEPS = 16
BLOCKS = L // STEPS
assert STEPS * B == 512

STEPS_START, STEPS_LN = 2, 2
STEPS_BEFORE = 24
STEPS_CHUNK = 6


class Count:

    def __init__(self):
        self.value = 0

    def up(self):
        self.value += 1
        return self.value


def build(nc, x, adj, we, wx, wh, bias, wqpk, pkeys, wq, kv, wo, out):
    fp32, bf16, u32, i32 = mybir.dt.float32, mybir.dt.bfloat16, mybir.dt.uint32, mybir.dt.int32
    ALU = mybir.AluOpType
    ACT = mybir.ActivationFunctionType
    X = mybir.AxisListType.X

    ctx = ExitStack()
    with ctx:
        def sb(name, shape, dt=fp32):
            return ctx.enter_context(nc.sbuf_tensor(name, shape, dt))

        def sem(name):
            return ctx.enter_context(nc.semaphore(name))

        we_sb, wx_sb, wh_sb = (sb(n, [128, D]) for n in ("we_sb", "wx_sb", "wh_sb"))
        bias_sb = sb("bias_sb", [128, 1])
        wqpk_sb = sb("wqpk_sb", [128, 8, 128])
        keys_bd = sb("keys_bd", [128, 2, 4, 2, NK])
        wq_sb = sb("wq_sb", [128, H, D])
        wo_sb = sb("wo_sb", [128, H, D])
        ident = sb("ident", [128, 128])
        identb = sb("identb", [128, 128], bf16)
        maskb = sb("maskb", [128, 128], bf16)
        iota_i = sb("iota_i", [128, H * TOP], i32)
        iota_c = sb("iota_c", [128, NC])
        rowbase = sb("rowbase", [128, H, TOP])
        eps = sb("eps", [128, 1])

        x_all = sb("x_all", [128, B * C, D])
        h_all = sb("h_all", [128, L, B])
        G = sb("G", [128, RING * SLOTS, 2 * D])
        diag = sb("diag", [128, 2, TOP, 128])
        KT = sb("KT", [128, H, L])
        V = sb("V", [128, H, C, D])
        adj_g = KT[:, :, :].rearrange("p (g r) m -> p g r m", g=2)
        v_flat = V[:, :, :, :].rearrange("p h c d -> p (h c) d")
        lnT_g = v_flat[:, 0:8, :].rearrange("p (g r) d -> p g r d", g=2)
        beta_g = v_flat[:, 8:16, :].rearrange("p (g r) d -> p g r d", g=2)
        sims = sb("sims", [128, 4, 2, 2, NK])
        xn_g = sims[:, 0:2, :, :, :].rearrange("p g a b k -> p g (a b) k")
        x_stats = sb("x_stats", [128, B * C, 6])
        mean, dmean, vsum, rstd = (sb(n, [128, B * C]) for n in ("mean", "dmean", "vsum", "rstd"))
        norm_g = sb("norm_g", [128, 2, 2 * C])
        rnorm_g = sb("rnorm_g", [128, 2, 2 * C])

        yT = sb("yT", [128, 128])
        x1 = sb("x1", [128, C, D])
        stats = sb("stats", [128, 6])
        mv = sb("mv", [128, 2])
        std = sb("std", [128, 1])
        rs = sb("rs", [128, 1])
        ln = sb("ln", [128, D])
        lnT = sb("lnT", [128, 128])
        qpkT = sb("qpkT", [128, 8, 128])
        qT = sb("qT", [128, C, H, 128])
        spare = sb("spare", [128, 4, NK])
        S1 = sb("S1", [128, 2, H, TOP])
        I1 = sb("I1", [128, 2, H, TOP], u32)
        I1f = sb("I1f", [128, 2, H, TOP])
        CV = sb("CV", [128, H, NC])
        CI = sb("CI", [128, H, NC])
        S2 = sb("S2", [128, H, TOP])
        P2 = sb("P2", [128, H, TOP], u32)
        P2f = sb("P2f", [128, H, TOP])
        hot = sb("hot", [128, 2, TOP, NC])
        h_ring = hot[:, :, :, :].rearrange("p a k n -> p (a k n)")[:, 0:2 * STEPS * B] \
            .rearrange("p (s b) -> p s b", b=B)
        rowf = sb("rowf", [128, H, TOP])
        idx = sb("idx", [128, C, H * TOP], u32)
        wexp = sb("wexp", [128, H, TOP])
        wsum = sb("wsum", [128, H])
        w = sb("w", [128, C, H, TOP])
        nmax = sb("nmax", [128, 2])
        rsum = sb("rsum", [128, 2])
        rrec = sb("rrec", [128, 2])
        P = sb("P", [128, 2, L])
        PT = sb("PT", [128, C, 128])
        oT = sb("oT", [128, 128])
        y = sb("y", [128, C, D])

        bank = [ctx.enter_context(nc.psum_tensor(f"bank{i}", [128, 512], fp32)) for i in range(8)]
        kv_ps, score_ps, pT_ps, wo_ps = bank[0:4]
        o_ps = pT_ps[:, 256:512]
        ident_ps = bank[4][:, 0:128]
        z_ps = bank[5:7]
        fill = bank[6:8]
        const_landed = sem("const_landed")
        weights_landed = sem("weights_landed")
        x_landed = [sem(f"x_landed{q}") for q in range(4)]
        adj_landed = [sem(f"adj_landed{g}") for g in range(2)]
        consts = sem("consts")
        bases_read = sem("bases_read")
        setup = sem("setup")
        ident_copied = sem("ident_copied")
        v_chain = sem("v_chain")
        vars_ready = sem("vars_ready")
        std_all = sem("std_all")
        xn_ready = sem("xn_ready")
        norm_ready = sem("norm_ready")
        xnT_done = sem("xnT_done")
        lnTg_ready = sem("lnTg_ready")
        beta_done = sem("beta_done")
        betag_ready = sem("betag_ready")
        agg_done = sem("agg_done")
        agg_ready = sem("agg_ready")
        h_ready = sem("h_ready")
        z_done = sem("z_done")
        h_copied = sem("h_copied")

        landed = [sem(f"landed{s}") for s in range(RING)]
        gate = sem("gate")
        ws_done = sem("ws_done")
        diag_ready = sem("diag_ready")
        idx_ready = sem("idx_ready")
        kv_ready = sem("kv_ready")
        scores_done = sem("scores_done")
        max_ready = sem("max_ready")
        exp_ready = sem("exp_ready")
        p_ready = sem("p_ready")
        pT_done = sem("pT_done")
        pT_ready = sem("pT_ready")
        o_done = sem("o_done")
        oT_ready = sem("oT_ready")
        wo_done = sem("wo_done")
        y_ready = sem("y_ready")
        stored = [sem(f"stored{c}") for c in range(C)]
        yT_ready = sem("yT_ready")
        yback_done = sem("yback_done")
        mv_ready = sem("mv_ready")
        std_ready = sem("std_ready")
        ln_ready = sem("ln_ready")
        lnT_done = sem("lnT_done")
        lnT_ready = sem("lnT_ready")
        fill_done = sem("fill_done")
        fill_ready = sem("fill_ready")
        gaps = sem("gaps")
        gexp = sem("gexp")

        NG = B // 2
        block = ctx.enter_context(nc.Block())

        PLAN = [[0], [1], [2], [3], [4], [5], [], []]
        FIRST_PLAN = [[], [], [], [], [0, 1], [2, 3], [4], [5]]

        @block.sync
        def _(sp):
            for q in range(4):
                sp.dma_start(x_all[:, 16 * q:16 * q + 16, :],
                             x[8 * q:8 * q + 8].rearrange("b (c p) d -> p (b c) d", p=128)).then_inc(x_landed[q], 16)
            sp.sem_inc(agg_done, 2)
            with sp.Fori(0, NG // 2) as i:
                for g in range(2):
                    sp.wait_ge(agg_done, i * 2 + (g + 1))
                    for k in range(2):
                        sp.dma_start(adj_g[:, g, 2 * k:2 * k + 2, :],
                                     adj[bass.ds(i * 4 + (2 * g + k), 1)]
                                     .rearrange("b (c p) m -> p (b c) m", p=128)).then_inc(adj_landed[g], 16)

            def store(n, c):
                sp.wait_ge(y_ready, n * 2 + (c + 2))
                sp.dma_start(out[bass.ds(n, 1), 128 * c:128 * c + 128, :].rearrange("b p d -> p (b d)"),
                             y[:, c, :]).then_inc(stored[c], 16)

            with sp.Fori(0, B) as n:
                for c in range(C):
                    store(n, c)
            for c in range(C):
                sp.wait_ge(stored[c], 16 * (B + 1))

        @block.gpsimd
        def _(pool):
            pool.memset(ident[:, :], 0.0).then_inc(consts, 1)
            pool.memset(identb[:, :], 0.0).then_inc(consts, 1)
            pool.memset(maskb[:, :], 0.0).then_inc(consts, 1)
            pool.memset(h_ring[:, 2 * STEPS - 1, :], 0.0).then_inc(consts, 1)
            pool.memset(eps[:, :], EPS_LN).then_inc(consts, 1)
            pool.iota(iota_i[:, :], pattern=[[NKV, H], [0, TOP]], base=0, channel_multiplier=0).then_inc(consts, 1)
            pool.wait_ge(consts, 3)
            for m in (ident, identb):
                pool.affine_select(out=m[:, :], in_=m[:, :], compare_op=ALU.not_equal, fill=1.0,
                                   base=0, pattern=[[-1, 128]], channel_multiplier=1).then_inc(consts, 1)
            pool.affine_select(out=maskb[:, :], in_=maskb[:, :], compare_op=ALU.is_ge, fill=LOWEST,
                               base=0, pattern=[[-1, 128]], channel_multiplier=1).then_inc(consts, 1)
            pool.wait_ge(bases_read, 1)
            pool.iota(iota_i[:, 0:NC], pattern=[[1, NC]], base=0, channel_multiplier=0).then_inc(consts, 1)

            def gather(n, c):
                for h in range(H):
                    if h % 2 == 0:
                        pool.wait_ge(idx_ready, n * (C * H // 2) + ((c * H + h) // 2 + 1))
                        pool.sem_inc(gate, 1)
                    for k in range(CHUNKS):
                        slot = (h % 2) * CHUNKS + k
                        pool.wait_ge(ws_done, n * (C * H * CHUNKS) + ((c * H + h) * CHUNKS + k + 1))
                        pool.sem_inc(gate, 1)
                        for s in range(SLOTS):
                            col = h * TOP + k * SLOTS + s
                            pool.indirect_dma_start(
                                G[:, slot * SLOTS + s, :], None, kv,
                                bass.IndirectOffsetOnAxis(idx[:, c, col:col + 1], 0)).then_inc(landed[slot], 16)

            with pool.Fori(0, B) as n:
                for c in range(C):
                    gather(n, c)

        @block.scalar
        def _(act):
            for dst, src in ((we_sb[:, :], we), (wx_sb[:, :], wx), (wh_sb[:, :], wh),
                             (bias_sb[:, :], bias.rearrange("(p a) -> p a", a=1))):
                act.dma_start(dst, src).then_inc(const_landed, 16)
            act.wait_ge(consts, 9)
            nc.scalar.activation(ident_ps, ident[:, :], ACT.Copy).then_inc(ident_copied, 1)
            act.wait_ge(vars_ready, 1)
            nc.scalar.activation(rstd[:, :], vsum[:, :], ACT.Sqrt, bias=eps[:, :], scale=1.0 / D).then_inc(std_all, 1)

            with act.Fori(0, NG // 2) as i:
                for g in range(2):
                    act.wait_ge(xnT_done, i * 2 + (g + 1))
                    nc.scalar.activation(lnT_g[:, g].rearrange("p r d -> p (r d)"), bank[0][:, :],
                                         ACT.Copy).then_inc(lnTg_ready, 1)
                    act.wait_ge(norm_ready, i * 2 + (g + 1))
                    act.sem_inc(gate, 1)
                    act.wait_ge(beta_done, i * 2 + (g + 1))
                    for r in range(2 * C):
                        nc.scalar.activation(beta_g[:, g, r, :], bank[1][:, 128 * r:128 * r + 128],
                                             ACT.Copy, scale=rnorm_g[:, g, r:r + 1]).then_inc(betag_ready, 1)

            act.wait_ge(setup, 2)
            for half in range(2):
                for hh in range(2):
                    act.dma_start(keys_bd[DK * hh:DK * hh + DK, half, :, hh, :],
                                  pkeys[DK * hh:DK * hh + DK, half]).then_inc(weights_landed, 16)
            for dst, src in ((wqpk_sb[:, :, :].rearrange("p a b -> p (a b)"), wqpk),
                             (wq_sb[:, :, :].rearrange("p a b -> p (a b)"), wq),
                             (wo_sb[:, :, :], wo.rearrange("(h p) d -> p h d", p=128))):
                act.dma_start(dst, src).then_inc(weights_landed, 16)

            act.wait_ge(const_landed, 64)
            act.sem_inc(h_copied, 2)
            with act.Fori(0, BLOCKS // 4) as i:
                for k in range(2):
                    act.wait_ge(h_copied, i * 2 + (k + 1))
                    act.sem_inc(gate, 1)
                    for s in range(STEPS):
                        act.wait_ge(z_done, i * (2 * STEPS) + (k * STEPS + s + 1))
                        nc.scalar.activation(h_ring[:, k * STEPS + s, :], z_ps[k][:, B * s:B * s + B],
                                             ACT.Tanh, bias=bias_sb[:, :]).then_inc(h_ready, 1)

            later_steps = iter(range(L // 2, L))

            def recur(count):
                for t in itertools.islice(later_steps, count):
                    s = t % STEPS
                    act.wait_ge(z_done, t + 1)
                    nc.scalar.activation(h_all[:, t, :], z_ps[t // STEPS % 2][:, B * s:B * s + B],
                                         ACT.Tanh, bias=bias_sb[:, :]).then_inc(h_ready, 1)

            def evac_kv(n, c, h):
                u = C * H
                for k, (dst, src) in enumerate(((KT[:, h, 128 * c:128 * c + 128], kv_ps[:, 0:128]),
                                                (V[:, h, c, :], kv_ps[:, 128:256]))):
                    if k == 0:
                        act.wait_ge(ws_done, n * (u * CHUNKS) + ((c * H + h + 1) * CHUNKS + RING))
                    nc.scalar.activation(dst, src, ACT.Copy).then_inc(kv_ready, 1)

            def evac_attention(n, c, h):
                j = c * H + h
                act.wait_ge(pT_done, n * (C * H) + (j + 1))
                nc.scalar.activation(PT[:, 0:c + 1, :], pT_ps[:, 0:128 * (c + 1)].rearrange("p (a i) -> p a i", i=128),
                                     ACT.Copy).then_inc(pT_ready, 1)
                act.wait_ge(o_done, n * (C * H) + (j + 1))
                nc.scalar.activation(oT[:, :], o_ps[:, 0:128], ACT.Copy).then_inc(oT_ready, 1)

            def exponential(n, c, h):
                act.wait_ge(max_ready, n * (C * H) + (c * H + h + 1))
                nc.scalar.activation(P[:, h % 2, 0:128 * (c + 1)], score_ps[:, 0:128 * (c + 1)], ACT.Exp,
                                     bias=nmax[:, h % 2:h % 2 + 1],
                                     accum_out=rsum[:, h % 2:h % 2 + 1]).then_inc(exp_ready, 1)

            def evac_fill(n, c, f, dst, scale=1.0):
                act.wait_ge(fill_done, n * (8 * C) + (8 * c + f + 1))
                nc.scalar.activation(dst, fill[f % 2][:, :], ACT.Copy, scale=scale).then_inc(fill_ready, 1)

            def route(n, c, step, first=False):
                if step == 0:
                    if first:
                        recur(STEPS_LN)
                    act.wait_ge(mv_ready, n * 2 + (c + 1))
                    nc.scalar.activation(std[:, :], mv[:, 1:2], ACT.Sqrt, bias=eps[:, :]).then_inc(std_ready, 1)
                    act.wait_ge(lnT_done, n * 2 + (c + 1))
                    nc.scalar.activation(lnT[:, :], fill[1][:, 128:256], ACT.Copy).then_inc(lnT_ready, 1)
                    for f in range(2):
                        evac_fill(n, c, f, qpkT[:, 4 * f:4 * f + 4, :].rearrange("p a t -> p (a t)"))
                    for f in range(2):
                        evac_fill(n, c, 2 + f, qT[:, c, 4 * f:4 * f + 4, :].rearrange("p a t -> p (a t)"),
                                  float(D) ** -0.5)
                if step in (1, 2):
                    for hp in (2 * step - 2, 2 * step - 1):
                        evac_fill(n, c, 4 + hp, sims[:, hp].rearrange("p a b k -> p (a b k)"))
                if step == 3:
                    act.wait_ge(gaps, n * 2 + (c + 1))
                    nc.scalar.activation(wexp[:, :, :], wexp[:, :, :], ACT.Exp).then_inc(gexp, 1)

            def tile(n, c, nxt, plan=PLAN, first=False):
                for h in range(H):
                    if first:
                        recur(STEPS_CHUNK * CHUNKS)
                    evac_kv(n, c, h)
                    if h:
                        evac_attention(n, c, h - 1)
                    exponential(n, c, h)
                    if nxt is not None:
                        for step in plan[h]:
                            route(*nxt, step)
                evac_attention(n, c, H - 1)

            recur(STEPS_START)
            for step in range(3):
                route(0, 0, step, first=True)
            recur(STEPS - STEPS_START - STEPS_LN + STEPS_BEFORE // 2)
            route(0, 0, 3)
            recur(STEPS_BEFORE - STEPS_BEFORE // 2)
            tile(0, 0, (0, 1), FIRST_PLAN, first=True)
            with act.Fori(0, B - 1) as n:
                tile(n, 1, (n + 1, 0))
                tile(n + 1, 0, (n + 1, 1))
            tile(B - 1, 1, None)

        @block.tensor
        def _(pe):
            pe.wait_ge(const_landed, 64)
            pe.wait_ge(consts, 10)

            def transpose_x(i, g):
                pe.wait_ge(xn_ready, i * (4 * C) + (2 * C * (g + 1)))
                for r in range(2 * C):
                    last = nc.tensor.transpose(bank[0][:, 128 * r:128 * r + 128], xn_g[:, g, r, :], ident[:, :])
                last.then_inc(xnT_done, 1)

            def beta(i, g):
                pe.wait_ge(lnTg_ready, i * 2 + (g + 1))
                for r in range(2 * C):
                    last = nc.tensor.matmul(bank[1][:, 128 * r:128 * r + 128], lnT_g[:, g, r, :], we_sb[:, :],
                                            start=True, stop=True)
                last.then_inc(beta_done, 1)

            def graph_product(i, g):
                pe.wait_ge(agg_ready, i * 2 + (g + 1))
                pe.sem_inc(gate, 1)
                pe.wait_ge(betag_ready, i * (4 * C) + (2 * C * (g + 1)))
                for k in range(2):
                    for c in range(C):
                        last = nc.tensor.matmul(bank[2 + g][:, L * k:L * k + L], beta_g[:, g, C * k + c, :],
                                                adj_g[:, g, C * k + c, :], start=(c == 0), stop=(c == C - 1))
                last.then_inc(agg_done, 1)

            transpose_x(0, 0)
            beta(0, 0)
            with pe.Fori(0, NG // 2 - 1) as i:
                for g in range(2):
                    transpose_x(i + g, 1 - g)
                    graph_product(i, g)
                    beta(i + g, 1 - g)
            transpose_x(NG // 2 - 1, 1)
            graph_product(NG // 2 - 1, 0)
            beta(NG // 2 - 1, 1)
            graph_product(NG // 2 - 1, 1)

            def input_product(bank_no, block):
                nc.tensor.matmul(z_ps[bank_no][:, :], wx_sb[:, :],
                                 h_all[:, bass.ds(block * STEPS, STEPS), :].rearrange("p t b -> p (t b)"),
                                 start=True, stop=True)

            pe.wait_ge(agg_ready, NG + 2)
            input_product(0, 0)
            pe.sem_inc(h_ready, 1)
            with pe.Fori(0, BLOCKS // 4) as i:
                for k in range(2):
                    for s in range(STEPS):
                        pe.wait_ge(h_ready, i * (2 * STEPS) + (k * STEPS + s + 1))
                        nc.tensor.matmul(z_ps[k][:, B * s:B * s + B], wh_sb[:, :],
                                         h_ring[:, (k * STEPS + s - 1) % (2 * STEPS), :],
                                         start=False, stop=True, skip_group_check=True).then_inc(z_done, 1)
                        if s == 1:
                            input_product(1 - k, i * 2 + (k + 1))

            later_steps = iter(range(L // 2, L))

            def recur(count):
                for t in itertools.islice(later_steps, count):
                    b, s = divmod(t, STEPS)
                    pe.wait_ge(h_ready, t + 1)
                    nc.tensor.matmul(z_ps[b % 2][:, B * s:B * s + B], wh_sb[:, :],
                                     h_ring[:, 2 * STEPS - 1, :] if t == L // 2 else h_all[:, t - 1, :],
                                     start=False, stop=True, skip_group_check=True).then_inc(z_done, 1)
                    if s == 1 and BLOCKS // 2 < b < BLOCKS - 1:
                        input_product((b + 1) % 2, b + 1)

            pe.wait_ge(weights_landed, 7 * 16)
            pe.wait_ge(setup, 2)
            pe.sem_inc(ws_done, RING)
            pe.sem_inc(kv_ready, 2)
            pe.sem_inc(exp_ready, 1)
            pe.sem_inc(y_ready, 1)
            pe.sem_inc(fill_ready, 2)

            def weighted_sums(n, c, h, first=False):
                j = c * H + h
                pe.wait_ge(diag_ready, n * (C * H) + (j + 1))
                pe.sem_inc(gate, 1)
                pe.wait_ge(kv_ready, n * (2 * C * H) + (2 * j + 2))
                pe.sem_inc(gate, 1)
                for k in range(CHUNKS):
                    slot = (h % 2) * CHUNKS + k
                    pe.wait_ge(landed[slot], n * (C * H // 2 * SLOTS * 16) + (j // 2 + 1) * SLOTS * 16)
                    for s in range(k * SLOTS, k * SLOTS + SLOTS):
                        at = (h % 2) * TOP + s
                        nc.tensor.matmul(kv_ps[:, 0:128], G[:, at, 0:D], diag[:, h % 2, s, :],
                                         start=(s == 0), stop=(s == TOP - 1), skip_group_check=True)
                        last = nc.tensor.matmul(kv_ps[:, 128:256], diag[:, h % 2, s, :], G[:, at, D:2 * D],
                                                start=False, stop=(s == TOP - 1), skip_group_check=True)
                        if first and s % SLOTS < SLOTS - 1:
                            recur(STEPS_CHUNK // (SLOTS - 1))
                    last.then_inc(ws_done, 1)

            def scores(n, c, h):
                j = c * H + h
                pe.wait_ge(exp_ready, n * (C * H) + (j + 1))
                own = score_ps[:, 128 * c:128 * c + 128]
                nc.tensor.matmul(own, identb[:, :], maskb[:, :], start=True, stop=False)
                pe.wait_ge(kv_ready, n * (2 * C * H) + (2 * j + 4))
                last = nc.tensor.matmul(own, qT[:, c, h, :], KT[:, h, 128 * c:128 * c + 128], start=False, stop=True)
                if c:
                    last = nc.tensor.matmul(score_ps[:, 0:128], qT[:, c, h, :], KT[:, h, 0:128], start=True, stop=True)
                last.then_inc(scores_done, 1)

            def attention(n, c, h):
                j = c * H + h
                pe.wait_ge(p_ready, n * (C * H) + (j + 1))
                for a in range(c + 1):
                    last = nc.tensor.transpose(pT_ps[:, 128 * a:128 * a + 128], P[:, h % 2, 128 * a:128 * a + 128],
                                               ident[:, :])
                last.then_inc(pT_done, 1)
                pe.wait_ge(pT_ready, n * (C * H) + (j + 1))
                for a in range(c + 1):
                    last = nc.tensor.matmul(o_ps[:, 0:128], V[:, h, a, :], PT[:, a, :], start=(a == 0), stop=(a == c))
                last.then_inc(o_done, 1)
                if h == 0:
                    pe.wait_ge(y_ready, n * 2 + (c + 1))
                    pe.sem_inc(gate, 1)
                pe.wait_ge(oT_ready, n * (C * H) + (j + 1))
                last = nc.tensor.matmul(wo_ps[:, 0:128], oT[:, :], wo_sb[:, h, :], start=(h == 0), stop=(h == H - 1))
                if h == H - 1:
                    last.then_inc(wo_done, 1)

            def fill_bank(n, c, f, products):
                pe.wait_ge(fill_ready, n * (8 * C) + (8 * c + f + 1))
                for at, lhsT, rhs in products:
                    last = nc.tensor.matmul(fill[f % 2][:, at], lhsT, rhs, start=True, stop=True)
                last.then_inc(fill_done, 1)

            def route(n, c, step, first=False):
                if step == 0:
                    pe.wait_ge(fill_ready, n * (8 * C) + (8 * c + 2))
                    pe.sem_inc(gate, 1)
                    pe.wait_ge(yT_ready, n * 2 + (c + 1))
                    nc.tensor.transpose(fill[1][:, 0:128], yT[:, :], ident[:, :]).then_inc(yback_done, 1)
                    if first:
                        recur(STEPS_LN)
                    pe.wait_ge(ln_ready, n * 2 + (c + 1))
                    nc.tensor.transpose(fill[1][:, 128:256], ln[:, :], ident[:, :]).then_inc(lnT_done, 1)
                    pe.wait_ge(lnT_ready, n * 2 + (c + 1))
                    for f in range(2):
                        fill_bank(n, c, f, [(slice(128 * a, 128 * a + 128), wqpk_sb[:, 4 * f + a, :], lnT[:, :])
                                            for a in range(4)])
                    for f in range(2):
                        fill_bank(n, c, 2 + f, [(slice(128 * a, 128 * a + 128), wq_sb[:, 4 * f + a, :], lnT[:, :])
                                                for a in range(4)])
                if step in (1, 2):
                    for hp in (2 * step - 2, 2 * step - 1):
                        fill_bank(n, c, 4 + hp, [(slice(256 * half, 256 * half + 256), qpkT[:, 4 * half + hp, :],
                                                  keys_bd[:, half, hp, :, :].rearrange("p a k -> p (a k)"))
                                                 for half in range(2)])

            def tile(n, c, nxt, plan=PLAN, first=False):
                for h in range(H):
                    weighted_sums(n, c, h, first)
                    scores(n, c, h)
                    if h:
                        attention(n, c, h - 1)
                    if nxt is not None:
                        if first and 0 in plan[h]:
                            pe.wait_ge(h_ready, L + 1)
                            pe.sem_inc(gate, 1)
                        for step in plan[h]:
                            route(*nxt, step)
                attention(n, c, H - 1)

            recur(STEPS_START)
            for step in range(3):
                route(0, 0, step, first=True)
            recur(STEPS - STEPS_START - STEPS_LN)
            pe.wait_ge(fill_ready, 8 + 2)
            input_product(1, BLOCKS // 2 + 1)
            recur(STEPS_BEFORE)
            tile(0, 0, (0, 1), FIRST_PLAN, first=True)
            with pe.Fori(0, B - 1) as n:
                tile(n, 1, (n + 1, 0))
                tile(n + 1, 0, (n + 1, 1))
            tile(B - 1, 1, None)

        @block.vector
        def _(dve):
            chain = Count()

            def follow():
                dve.wait_ge(v_chain, chain.value)

            def clear_chain():
                follow()
                dve.sem_clear(v_chain)
                chain.value = 0

            dve.wait_ge(consts, 6)
            nc.vector.tensor_copy(rowbase[:, :, :].rearrange("p h k -> p (h k)"), iota_i[:, :]).then_inc(bases_read, 1)
            nc.vector.memset(keys_bd[:, 0, :, :, :], 0.0).then_inc(setup, 1)
            nc.vector.memset(keys_bd[:, 1, :, :, :], 0.0).then_inc(setup, 1)
            dve.wait_ge(consts, 10)
            nc.vector.tensor_copy(iota_c[:, :], iota_i[:, 0:NC]).then_inc(v_chain, 1)
            chain.up()

            for q in range(4):
                dve.wait_ge(x_landed[q], 16)
                with dve.Fori(4 * q, 4 * q + 4) as i:
                    for r in range(4):
                        nc.vector.bn_stats(x_stats[:, bass.ds(i * 4 + r, 1), :].rearrange("p r s -> p (r s)"),
                                           x_all[:, bass.ds(i * 4 + r, 1), :].rearrange("p r d -> p (r d)")
                                           ).then_inc(v_chain, 1)
            chain.value += B * C
            follow()
            mean_even, mean_odd = x_stats[:, :, 1], x_stats[:, :, 4]
            nc.vector.tensor_tensor(dmean[:, :], mean_even, mean_odd, ALU.subtract).then_inc(v_chain, 1)
            chain.up()
            nc.vector.tensor_tensor(vsum[:, :], x_stats[:, :, 2], x_stats[:, :, 5], ALU.add).then_inc(v_chain, 1)
            chain.up()
            nc.vector.tensor_tensor(mean[:, :], mean_even, mean_odd, ALU.add).then_inc(v_chain, 1)
            chain.up()
            follow()
            nc.vector.tensor_tensor(dmean[:, :], dmean[:, :], dmean[:, :], ALU.mult).then_inc(v_chain, 1)
            chain.up()
            nc.vector.tensor_scalar(mean[:, :], mean[:, :], 0.5, None, ALU.mult).then_inc(v_chain, 1)
            chain.up()
            follow()
            nc.vector.scalar_tensor_tensor(vsum[:, :], dmean[:, :], D / 4.0, vsum[:, :],
                                           ALU.mult, ALU.add).then_inc(vars_ready, 1)
            dve.wait_ge(std_all, 1)
            nc.vector.reciprocal(rstd[:, :], rstd[:, :]).then_inc(v_chain, 1)
            chain.up()
            clear_chain()

            dve.sem_inc(agg_ready, 2)

            def normalise_group(i, g):
                for r in range(2 * C):
                    row = bass.ds(i * 8 + (4 * g + r), 1)
                    nc.vector.tensor_scalar(xn_g[:, g, r, :], x_all[:, row, :].rearrange("p r d -> p (r d)"),
                                            mean[:, row], rstd[:, row], ALU.subtract, ALU.mult).then_inc(xn_ready, 1)
                dve.wait_ge(adj_landed[g], i * 32 + 32)
                nc.vector.reduce_sum(norm_g[:, g, :], adj_g[:, g, :, :], axis=X).then_inc(v_chain, 1)
                chain.up()
                follow()
                nc.vector.tensor_scalar(norm_g[:, g, :], norm_g[:, g, :], EPS_NORM, None,
                                        ALU.max).then_inc(v_chain, 1)
                chain.up()
                follow()
                nc.vector.reciprocal(rnorm_g[:, g, :], norm_g[:, g, :]).then_inc(norm_ready, 1)

            def evacuate_product(i, g):
                dve.wait_ge(agg_done, i * 2 + (g + 3))
                dve.sem_inc(gate, 1)
                nc.vector.tensor_copy(
                    h_all[:, :, bass.ds(i * 4 + 2 * g, 2)].rearrange("p t b -> p b t"),
                    bank[2 + g][:, :].rearrange("p (b t) -> p b t", b=2)).then_inc(agg_ready, 1)

            normalise_group(0, 0)
            clear_chain()
            with dve.Fori(0, NG // 2 - 1) as i:
                for g in range(2):
                    normalise_group(i + g, 1 - g)
                    evacuate_product(i, g)
                clear_chain()
            normalise_group(NG // 2 - 1, 1)
            for g in range(2):
                evacuate_product(NG // 2 - 1, g)
            clear_chain()

            with dve.Fori(0, BLOCKS // 4) as i:
                for k in range(2):
                    dve.wait_ge(h_ready, i * (2 * STEPS) + (k + 1) * STEPS + 1)
                    dve.sem_inc(gate, 1)
                    nc.vector.tensor_copy(
                        h_all[:, bass.ds(i * (2 * STEPS) + k * STEPS, STEPS), :],
                        h_ring[:, k * STEPS:k * STEPS + STEPS, :]).then_inc(h_copied, 1)
            dve.wait_ge(h_copied, BLOCKS // 2 + 2)
            for c in range(C):
                dve.sem_inc(stored[c], 16)

            def diagonal(n, c, h):
                dve.wait_ge(ws_done, n * (C * H * CHUNKS) + ((c * H + h - 1) * CHUNKS + RING))
                dve.sem_inc(gate, 1)
                nc.vector.tensor_tensor(diag[:, h % 2, :, :],
                                        ident_ps.unsqueeze(1).broadcast_to([128, TOP, 128]),
                                        w[:, c, h, :].unsqueeze(2).broadcast_to([128, TOP, 128]),
                                        ALU.mult).then_inc(diag_ready, 1)

            def row_max(n, c, h):
                dve.wait_ge(scores_done, n * (C * H) + (c * H + h + 1))
                nc.vector.tensor_reduce(nmax[:, h % 2:h % 2 + 1], score_ps[:, 0:128 * (c + 1)], axis=X, op=ALU.max,
                                        negate=True).then_inc(max_ready, 1)

            def normalise(n, c, h):
                dve.wait_ge(exp_ready, n * (C * H) + (c * H + h + 2))
                nc.vector.reciprocal(rrec[:, h % 2:h % 2 + 1], rsum[:, h % 2:h % 2 + 1]).then_inc(v_chain, 1)
                chain.up()
                follow()
                nc.vector.tensor_scalar(P[:, h % 2, 0:128 * (c + 1)], P[:, h % 2, 0:128 * (c + 1)],
                                        rrec[:, h % 2:h % 2 + 1], None, ALU.mult).then_inc(p_ready, 1)

            def top16(jobs):
                marks = []
                for src, _, best, _ in jobs:
                    nc.vector.max(best[:, 0:8], src).then_inc(v_chain, 1)
                    marks.append(chain.up())
                for j, (src, rest, best, at) in enumerate(jobs):
                    dve.wait_ge(v_chain, marks[j])
                    nc.vector.match_replace(rest, best[:, 0:8], src, REPLACED).then_inc(v_chain, 1)
                    marks[j] = chain.up()
                    nc.vector.max_index(at[:, 0:8], best[:, 0:8], src).then_inc(v_chain, 1)
                    chain.up()
                for j, (_, rest, best, _) in enumerate(jobs):
                    dve.wait_ge(v_chain, marks[j])
                    nc.vector.max(best[:, 8:16], rest).then_inc(v_chain, 1)
                    marks[j] = chain.up()
                for j, (_, rest, best, at) in enumerate(jobs):
                    dve.wait_ge(v_chain, marks[j])
                    nc.vector.max_index(at[:, 8:16], best[:, 8:16], rest).then_inc(v_chain, 1)
                    chain.up()

            def layernorm(n, c):
                nc.vector.tensor_copy(yT[:, :], h_all[:, 128 * c:128 * c + 128, bass.ds(n, 1)]
                                      .rearrange("p t b -> p (t b)")).then_inc(yT_ready, 1)
                dve.wait_ge(yback_done, n * 2 + (c + 1))
                dve.sem_inc(gate, 1)
                nc.vector.tensor_tensor(x1[:, c, :], x_all[:, bass.ds(n * 2 + c, 1), :].rearrange("p r d -> p (r d)"),
                                        fill[1][:, 0:128], ALU.add).then_inc(v_chain, 1)
                chain.up()
                follow()
                nc.vector.bn_stats(stats[:, :], x1[:, c, :]).then_inc(v_chain, 1)
                chain.up()
                follow()
                nc.vector.bn_aggr(mv[:, :], stats[:, :]).then_inc(mv_ready, 1)
                dve.wait_ge(std_ready, n * 2 + (c + 1))
                nc.vector.reciprocal(rs[:, :], std[:, :]).then_inc(v_chain, 1)
                chain.up()
                follow()
                nc.vector.tensor_scalar(ln[:, :], x1[:, c, :], mv[:, 0:1], rs[:, :],
                                        ALU.subtract, ALU.mult).then_inc(ln_ready, 1)

            def half_keys(n, c, step):
                for hp in (2 * step - 2, 2 * step - 1):
                    dve.wait_ge(fill_ready, n * (8 * C) + (8 * c + 4 + hp + 3))
                    dve.sem_inc(gate, 1)
                    top16([(sims[:, hp, half, hh, :], spare[:, 2 * half + hh, :], S1[:, half, 2 * hp + hh, :],
                            I1[:, half, 2 * hp + hh, :]) for half in range(2) for hh in range(2)])

            def pairs(n, c):
                follow()
                nc.vector.tensor_tensor(I1f[:, 0], I1[:, 0], rowbase[:, :, :], ALU.add).then_inc(v_chain, 1)
                chain.up()
                nc.vector.tensor_scalar(I1f[:, 1], I1[:, 1], float(NK), None, ALU.mult).then_inc(v_chain, 1)
                chain.up()
                for dst, src in ((CV, S1), (CI, I1f)):
                    at = 0
                    if src is I1f:
                        follow()
                    for i0, ni, nj in PAIRS:
                        if ni == 1:
                            shape = [128, H, nj]
                            o = dst[:, :, at:at + nj]
                            a, b = src[:, 0, :, i0:i0 + 1].broadcast_to(shape), src[:, 1, :, 0:nj]
                        elif nj == 1:
                            shape = [128, H, ni]
                            o = dst[:, :, at:at + ni]
                            a, b = src[:, 0, :, i0:i0 + ni], src[:, 1, :, 0:1].broadcast_to(shape)
                        else:
                            shape = [128, H, ni, nj]
                            o = dst[:, :, at:at + ni * nj].rearrange("p h (i j) -> p h i j", j=nj)
                            a = src[:, 0, :, i0:i0 + ni].unsqueeze(3).broadcast_to(shape)
                            b = src[:, 1, :, 0:nj].unsqueeze(2).broadcast_to(shape)
                        nc.vector.tensor_tensor(o, a, b, ALU.add).then_inc(v_chain, 1)
                        chain.up()
                        at += ni * nj
                follow()
                for h0 in (0, 4):
                    top16([(CV[:, h, :], spare[:, h - h0, 0:NC], S2[:, h, :], P2[:, h, :])
                           for h in range(h0, h0 + 4)])
                follow()
                nc.vector.tensor_copy(P2f[:, :, :], P2[:, :, :]).then_inc(v_chain, 1)
                chain.up()
                nc.vector.tensor_tensor(wexp[:, :, :], S2[:, :, :], S2[:, :, 0:1].broadcast_to([128, H, TOP]),
                                        ALU.subtract).then_inc(gaps, 1)

            def table_rows(n, c, h0):
                hs = slice(h0, h0 + 2)
                shape = [128, 2, TOP, NC]
                follow()
                nc.vector.tensor_tensor(
                    hot[:, :, :, :], P2f[:, hs, :].unsqueeze(3).broadcast_to(shape),
                    iota_c[:, :].unsqueeze(1).unsqueeze(1).broadcast_to(shape), ALU.is_equal).then_inc(v_chain, 1)
                chain.up()
                follow()
                nc.vector.tensor_tensor(hot[:, :, :, :], hot[:, :, :, :],
                                        CI[:, hs, :].unsqueeze(2).broadcast_to(shape), ALU.mult).then_inc(v_chain, 1)
                chain.up()
                follow()
                nc.vector.reduce_sum(rowf[:, hs, :], hot[:, :, :, :], axis=X).then_inc(v_chain, 1)
                chain.up()
                follow()
                nc.vector.tensor_copy(idx[:, c, TOP * h0:TOP * h0 + 2 * TOP],
                                      rowf[:, hs, :].rearrange("p h k -> p (h k)")).then_inc(idx_ready, 1)

            def weights(n, c):
                dve.wait_ge(gexp, n * 2 + (c + 1))
                nc.vector.reduce_sum(wsum[:, :], wexp[:, :, :], axis=X).then_inc(v_chain, 1)
                chain.up()
                follow()
                nc.vector.reciprocal(wsum[:, :], wsum[:, :]).then_inc(v_chain, 1)
                chain.up()
                follow()
                nc.vector.tensor_tensor(w[:, c, :, :], wexp[:, :, :],
                                        wsum[:, :].unsqueeze(2).broadcast_to([128, H, TOP]),
                                        ALU.mult).then_inc(v_chain, 1)
                chain.up()

            def route(n, c, step):
                if step == 0:
                    layernorm(n, c)
                if step in (1, 2):
                    half_keys(n, c, step)
                if step == 3:
                    pairs(n, c)
                    weights(n, c)
                if step in (4, 5):
                    for h0 in (4 * step - 16, 4 * step - 14):
                        table_rows(n, c, h0)

            def tile(n, c, nxt, plan=PLAN, first=False):
                for h in range(H):
                    if h:
                        normalise(n, c, h - 1)
                    if h < H - 1:
                        diagonal(n, c, h + 1)
                    elif nxt is not None and not first:
                        diagonal(*nxt, 0)
                    row_max(n, c, h)
                    if nxt is not None:
                        if first and 0 in plan[h]:
                            dve.wait_ge(h_ready, L + 1)
                        for step in plan[h]:
                            route(*nxt, step)
                normalise(n, c, H - 1)
                if first:
                    diagonal(*nxt, 0)
                dve.wait_ge(stored[c], n * 16 + 16)
                dve.sem_inc(gate, 1)
                dve.wait_ge(wo_done, n * 2 + (c + 1))
                nc.vector.tensor_tensor(y[:, c, :], x1[:, c, :], wo_ps[:, 0:128], ALU.add).then_inc(y_ready, 1)
                clear_chain()

            dve.wait_ge(ident_copied, 1)
            for step in range(4):
                route(0, 0, step)
            table_rows(0, 0, 0)
            diagonal(0, 0, 0)
            for h0 in (2, 4, 6):
                table_rows(0, 0, h0)
            clear_chain()
            tile(0, 0, (0, 1), FIRST_PLAN, first=True)
            with dve.Fori(0, B - 1) as n:
                tile(n, 1, (n + 1, 0))
                tile(n + 1, 0, (n + 1, 1))
            tile(B - 1, 1, None)


_ORDER = ["x", "adj", "L0_gnn_e_weight", "L0_gnn_Wx", "L0_gnn_Wh", "L0_gnn_b", "L0_ffn_Wq_pk",
          "pk_keys_t", "L0_ffn_Wq", "key_value_rows", "L0_ffn_Wo"]


def kernel(**inputs):
    import numpy as _np
    import concourse.bacc as _bacc
    from concourse import mybir as _mybir
    from concourse.bass_utils import run_bass_kernel_spmd as _run

    arrays = {k: _np.asarray(v) for k, v in inputs.items()}
    keys = arrays.pop("L0_ffn_pk_keys").transpose(2, 3, 0, 1).reshape(H // 2, 2 * DK, 2, NK)
    arrays["pk_keys_t"] = _np.ascontiguousarray(keys.transpose(1, 2, 0, 3))
    arrays["key_value_rows"] = _np.concatenate(
        [arrays.pop("L0_ffn_keys_table"), arrays.pop("L0_ffn_values_table")], axis=1)

    nc = _bacc.Bacc("TRN2", target_bir_lowering=False, num_devices=1)
    feeds, args = {}, []
    for name in _ORDER:
        a = _np.ascontiguousarray(arrays[name])
        feeds[f"in_{name}"] = a
        args.append(nc.dram_tensor(f"in_{name}", a.shape, _mybir.dt.from_np(a.dtype), kind="ExternalInput").ap())
    args.append(nc.dram_tensor("out_x", (B, L, D), _mybir.dt.float32, kind="ExternalOutput").ap())
    build(nc, *args)
    return _run(nc, [feeds], core_ids=[0]).results[0]["out_x"]
```

```python
import concourse.bass as bass
from concourse import mybir
from contextlib import ExitStack
import itertools


B, L, D = 32, 256, 128
H = 8
DK = D // 2
NK = 128
NKV = NK * NK
TOP = 16
C = L // 128
EPS_LN, EPS_NORM = 1e-5, 1e-7
LOWEST = -3.0e38
REPLACED = -3.4e38

PAIRS = [(0, 1, 16), (1, 1, 8), (2, 1, 5), (3, 1, 4), (4, 1, 3), (5, 3, 2), (8, 8, 1)]
NC = sum(ni * nj for _, ni, nj in PAIRS)
assert NC == sum(TOP // (i + 1) for i in range(TOP))

SLOTS = 4
CHUNKS = TOP // SLOTS
RING = 2 * CHUNKS
STEPS = 16
BLOCKS = L // STEPS
GROUPS = 4
assert STEPS * B == 512

STEPS_START, STEPS_LN = 2, 2
STEPS_BEFORE = 24
STEPS_CHUNK = 6


class Count:

    def __init__(self):
        self.value = 0

    def up(self):
        self.value += 1
        return self.value


def build(nc, x, adj, we, wx, wh, bias, wqpk, pkeys, wq, kv, wo, out):
    fp32, bf16, u32, i32 = mybir.dt.float32, mybir.dt.bfloat16, mybir.dt.uint32, mybir.dt.int32
    ALU = mybir.AluOpType
    ACT = mybir.ActivationFunctionType
    X = mybir.AxisListType.X

    ctx = ExitStack()
    with ctx:
        def sb(name, shape, dt=fp32):
            return ctx.enter_context(nc.sbuf_tensor(name, shape, dt))

        def sem(name):
            return ctx.enter_context(nc.semaphore(name))

        we_sb, wx_sb, wh_sb = (sb(n, [128, D]) for n in ("we_sb", "wx_sb", "wh_sb"))
        bias_sb = sb("bias_sb", [128, 1])
        wqpk_sb = sb("wqpk_sb", [128, 8, 128])
        keys_bd = sb("keys_bd", [128, 2, 4, 2, NK])
        wq_sb = sb("wq_sb", [128, H, D])
        wo_sb = sb("wo_sb", [128, H, D])
        ident = sb("ident", [128, 128])
        identb = sb("identb", [128, 128], bf16)
        maskb = sb("maskb", [128, 128], bf16)
        iota_i = sb("iota_i", [128, H * TOP], i32)
        rowbase = sb("rowbase", [128, H, TOP])
        eps = sb("eps", [128, 1])

        x_all = sb("x_all", [128, B * C, D])
        h_all = sb("h_all", [128, L, B])
        G = sb("G", [128, RING * SLOTS, 2 * D])
        diag = sb("diag", [128, 2, TOP, 128])
        KT = sb("KT", [128, H, L])
        V = sb("V", [128, H, C, D])
        adj_g = G[:, 0:GROUPS * 4, :].rearrange("p (g r) m -> p g r m", g=GROUPS)
        v_flat = V[:, :, :, :].rearrange("p h c d -> p (h c) d")
        lnT_g = v_flat[:, 0:8, :].rearrange("p (g r) d -> p g r d", g=2)
        beta_g = v_flat[:, 8:16, :].rearrange("p (g r) d -> p g r d", g=2)
        sims = sb("sims", [128, 4, 2, 2, NK])
        xn_g = sims[:, 0:2, :, :, :].rearrange("p g a b k -> p g (a b) k")
        x_stats = sb("x_stats", [128, 16, 6])
        dmean, vsum = (sb(n, [128, 16]) for n in ("dmean", "vsum"))
        mean, rstd = (sb(n, [128, 2, 16]) for n in ("mean", "rstd"))
        norm_g = sb("norm_g", [128, 2, 2 * C])
        rnorm_g = sb("rnorm_g", [128, 2, 2 * C])

        yT = sb("yT", [128, 128])
        x1 = sb("x1", [128, C, D])
        stats = sb("stats", [128, 6])
        mv = sb("mv", [128, 2])
        std = sb("std", [128, 1])
        rs = sb("rs", [128, 1])
        ln = sb("ln", [128, D])
        lnT = sb("lnT", [128, 128])
        qpkT = sb("qpkT", [128, 8, 128])
        qT = sb("qT", [128, C, H, 128])
        spare = sb("spare", [128, 4, NK])
        S1 = sb("S1", [128, 2, H, TOP])
        I1 = sb("I1", [128, 2, H, TOP], u32)
        I1f = sb("I1f", [128, 2, H, TOP])
        CV = sb("CV", [128, H, NC])
        CI = sb("CI", [128, H, NC])
        S2 = sb("S2", [128, H, TOP])
        P2 = sb("P2", [128, H, TOP], u32)
        P2f = sb("P2f", [128, H, TOP])
        hot = sb("hot", [128, 2, TOP, NC])
        h_ring = hot[:, :, :, :].rearrange("p a k n -> p (a k n)")[:, 0:2 * STEPS * B] \
            .rearrange("p (s b) -> p s b", b=B)
        rowf = sb("rowf", [128, H, TOP])
        idx = sb("idx", [128, C, H * TOP], u32)
        wexp = sb("wexp", [128, H, TOP])
        wsum = sb("wsum", [128, H])
        w = sb("w", [128, C, H, TOP])
        nmax = sb("nmax", [128, 2])
        rsum = sb("rsum", [128, 2])
        rrec = sb("rrec", [128, 2])
        P = sb("P", [128, 2, L])
        PT = sb("PT", [128, C, 128])
        oT = sb("oT", [128, 128])
        y = sb("y", [128, C, D])

        bank = [ctx.enter_context(nc.psum_tensor(f"bank{i}", [128, 512], fp32)) for i in range(8)]
        kv_ps, score_ps, pT_ps, wo_ps = bank[0:4]
        o_ps = pT_ps[:, 256:512]
        ident_ps = bank[4][:, 0:128]
        iota_ps = bank[4][:, 128:128 + NC]
        CI_ps = bank[4][:, 192:192 + 2 * NC].rearrange("p (h c) -> p h c", c=NC)
        z_ps = bank[5:7]
        fill = bank[6:8]
        const_landed = sem("const_landed")
        weights_landed = sem("weights_landed")
        x_first, x_rest = sem("x_first"), sem("x_rest")
        adj_landed = [sem(f"adj_landed{g}") for g in range(GROUPS)]
        consts = sem("consts")
        bases_read = sem("bases_read")
        setup = sem("setup")
        ident_copied = sem("ident_copied")
        v_chain = sem("v_chain")
        vars_ready = sem("vars_ready")
        std_all = sem("std_all")
        xn_ready = sem("xn_ready")
        norm_ready = sem("norm_ready")
        xnT_done = sem("xnT_done")
        lnTg_ready = sem("lnTg_ready")
        beta_done = sem("beta_done")
        betag_ready = sem("betag_ready")
        agg_done = sem("agg_done")
        agg_ready = sem("agg_ready")
        h_ready = sem("h_ready")
        z_done = sem("z_done")
        h_copied = sem("h_copied")

        landed = [sem(f"landed{s}") for s in range(RING)]
        gate = sem("gate")
        ws_done = sem("ws_done")
        diag_ready = sem("diag_ready")
        idx_ready = sem("idx_ready")
        kv_ready = sem("kv_ready")
        scores_done = sem("scores_done")
        max_ready = sem("max_ready")
        exp_ready = sem("exp_ready")
        p_ready = sem("p_ready")
        pT_done = sem("pT_done")
        pT_ready = sem("pT_ready")
        o_done = sem("o_done")
        oT_ready = sem("oT_ready")
        wo_done = sem("wo_done")
        y_ready = sem("y_ready")
        stored = [sem(f"stored{c}") for c in range(C)]
        yT_ready = sem("yT_ready")
        yback_done = sem("yback_done")
        mv_ready = sem("mv_ready")
        std_ready = sem("std_ready")
        ln_ready = sem("ln_ready")
        lnT_done = sem("lnT_done")
        lnT_ready = sem("lnT_ready")
        fill_done = sem("fill_done")
        fill_ready = sem("fill_ready")
        gaps = sem("gaps")
        gexp = sem("gexp")

        NG = B // 2
        X_TURN = 2 * GROUPS
        block = ctx.enter_context(nc.Block())

        PLAN = [[0], [1], [2], [3], [4], [5], [], []]
        FIRST_PLAN = [[], [], [], [0, 1], [2], [3, 4], [5], []]

        @block.sync
        def _(sp):
            sp.dma_start(x_all[:, 0:X_TURN * C, :],
                         x[0:X_TURN].rearrange("b (c p) d -> p (b c) d", p=128)).then_inc(x_first, 16)
            sp.sem_inc(agg_done, GROUPS)
            with sp.Fori(0, NG // GROUPS) as i:
                for g in range(GROUPS):
                    sp.wait_ge(agg_done, i * GROUPS + (g + 1))
                    for k in range(2):
                        sp.dma_start(adj_g[:, g, 2 * k:2 * k + 2, :],
                                     adj[bass.ds(i * (2 * GROUPS) + (2 * g + k), 1)]
                                     .rearrange("b (c p) m -> p (b c) m", p=128)).then_inc(adj_landed[g], 16)

            def store(n, c):
                sp.wait_ge(y_ready, n * 2 + (c + 2))
                sp.dma_start(out[bass.ds(n, 1), 128 * c:128 * c + 128, :].rearrange("b p d -> p (b d)"),
                             y[:, c, :]).then_inc(stored[c], 16)

            with sp.Fori(0, B) as n:
                for c in range(C):
                    store(n, c)
            for c in range(C):
                sp.wait_ge(stored[c], 16 * (B + 1))

        @block.gpsimd
        def _(pool):
            pool.memset(ident[:, :], 0.0).then_inc(consts, 1)
            pool.memset(identb[:, :], 0.0).then_inc(consts, 1)
            pool.memset(maskb[:, :], 0.0).then_inc(consts, 1)
            pool.memset(h_ring[:, 2 * STEPS - 1, :], 0.0).then_inc(consts, 1)
            pool.memset(eps[:, :], EPS_LN).then_inc(consts, 1)
            pool.iota(iota_i[:, :], pattern=[[NKV, H], [0, TOP]], base=0, channel_multiplier=0).then_inc(consts, 1)
            pool.wait_ge(consts, 3)
            for m in (ident, identb):
                pool.affine_select(out=m[:, :], in_=m[:, :], compare_op=ALU.not_equal, fill=1.0,
                                   base=0, pattern=[[-1, 128]], channel_multiplier=1).then_inc(consts, 1)
            pool.affine_select(out=maskb[:, :], in_=maskb[:, :], compare_op=ALU.is_ge, fill=LOWEST,
                               base=0, pattern=[[-1, 128]], channel_multiplier=1).then_inc(consts, 1)
            pool.wait_ge(bases_read, 1)
            pool.iota(iota_i[:, 0:NC], pattern=[[1, NC]], base=0, channel_multiplier=0).then_inc(consts, 1)

            def gather(n, c):
                for h in range(H):
                    if h % 2 == 0:
                        pool.wait_ge(idx_ready, n * (C * H // 2) + ((c * H + h) // 2 + 1))
                        pool.sem_inc(gate, 1)
                    for k in range(CHUNKS):
                        slot = (h % 2) * CHUNKS + k
                        pool.wait_ge(ws_done, n * (C * H * CHUNKS) + ((c * H + h) * CHUNKS + k + 1))
                        pool.sem_inc(gate, 1)
                        for s in range(SLOTS):
                            col = h * TOP + k * SLOTS + s
                            pool.indirect_dma_start(
                                G[:, slot * SLOTS + s, :], None, kv,
                                bass.IndirectOffsetOnAxis(idx[:, c, col:col + 1], 0)).then_inc(landed[slot], 16)

            with pool.Fori(0, B) as n:
                for c in range(C):
                    gather(n, c)

        @block.scalar
        def _(act):
            for dst, src in ((we_sb[:, :], we), (wx_sb[:, :], wx), (wh_sb[:, :], wh),
                             (bias_sb[:, :], bias.rearrange("(p a) -> p a", a=1))):
                act.dma_start(dst, src).then_inc(const_landed, 16)
            for b in range(X_TURN, B, X_TURN):
                act.dma_start(x_all[:, b * C:(b + X_TURN) * C, :],
                              x[b:b + X_TURN].rearrange("b (c p) d -> p (b c) d", p=128)).then_inc(x_rest, 16)
            act.wait_ge(consts, 9)
            nc.scalar.activation(ident_ps, ident[:, :], ACT.Copy).then_inc(ident_copied, 1)

            def deviation(i, par):
                act.wait_ge(vars_ready, i + 1)
                nc.scalar.activation(rstd[:, par, :], vsum[:, :], ACT.Sqrt, bias=eps[:, :],
                                     scale=1.0 / D).then_inc(std_all, 1)

            def evacuate_transposes(i, g):
                act.wait_ge(xnT_done, i * GROUPS + (g + 1))
                nc.scalar.activation(lnT_g[:, g % 2].rearrange("p r d -> p (r d)"), bank[0][:, :],
                                     ACT.Copy).then_inc(lnTg_ready, 1)

            def evacuate_beta(i, g):
                act.wait_ge(norm_ready, i * GROUPS + (g + 1))
                act.sem_inc(gate, 1)
                act.wait_ge(beta_done, i * GROUPS + (g + 1))
                for r in range(2 * C):
                    nc.scalar.activation(beta_g[:, g % 2, r, :], bank[1][:, 128 * r:128 * r + 128],
                                         ACT.Copy, scale=rnorm_g[:, g % 2, r:r + 1]).then_inc(betag_ready, 1)

            def evacuate_product(i, g):
                act.wait_ge(agg_done, i * GROUPS + (g + 1 + GROUPS))
                act.sem_inc(gate, 1)
                nc.scalar.activation(
                    h_all[:, :, bass.ds(i * (2 * GROUPS) + 2 * g, 2)].rearrange("p t b -> p b t"),
                    bank[2 + g % 2][:, :].rearrange("p (b t) -> p b t", b=2), ACT.Copy).then_inc(agg_ready, 1)

            def turn(i, last=False):
                for g in range(GROUPS):
                    if g == 2 and not last:
                        deviation(i + 1, 0)
                    if g < GROUPS - 1 or not last:
                        ahead = (i, g + 1) if g < GROUPS - 1 else (i + 1, 0)
                        evacuate_transposes(*ahead)
                    evacuate_product(i, g)
                    if g < GROUPS - 1 or not last:
                        evacuate_beta(*ahead)

            act.sem_inc(agg_ready, 2)
            deviation(0, 0)
            evacuate_transposes(0, 0)
            evacuate_beta(0, 0)
            with act.Fori(0, NG // GROUPS - 1) as i:
                turn(i)
            turn(NG // GROUPS - 1, last=True)

            act.wait_ge(setup, 2)
            for half in range(2):
                for hh in range(2):
                    act.dma_start(keys_bd[DK * hh:DK * hh + DK, half, :, hh, :],
                                  pkeys[DK * hh:DK * hh + DK, half]).then_inc(weights_landed, 16)
            for dst, src in ((wqpk_sb[:, :, :].rearrange("p a b -> p (a b)"), wqpk),
                             (wq_sb[:, :, :].rearrange("p a b -> p (a b)"), wq),
                             (wo_sb[:, :, :], wo.rearrange("(h p) d -> p h d", p=128))):
                act.dma_start(dst, src).then_inc(weights_landed, 16)

            act.wait_ge(const_landed, 64)
            act.sem_inc(h_copied, 2)
            with act.Fori(0, BLOCKS // 4) as i:
                for k in range(2):
                    act.wait_ge(h_copied, i * 2 + (k + 1))
                    act.sem_inc(gate, 1)
                    for s in range(STEPS):
                        act.wait_ge(z_done, i * (2 * STEPS) + (k * STEPS + s + 1))
                        nc.scalar.activation(h_ring[:, k * STEPS + s, :], z_ps[k][:, B * s:B * s + B],
                                             ACT.Tanh, bias=bias_sb[:, :]).then_inc(h_ready, 1)

            later_steps = iter(range(L // 2, L))

            def recur(count):
                for t in itertools.islice(later_steps, count):
                    s = t % STEPS
                    act.wait_ge(z_done, t + 1)
                    nc.scalar.activation(h_all[:, t, :], z_ps[t // STEPS % 2][:, B * s:B * s + B],
                                         ACT.Tanh, bias=bias_sb[:, :]).then_inc(h_ready, 1)

            def evac_kv(n, c, h):
                act.wait_ge(ws_done, n * (C * H * CHUNKS) + ((c * H + h + 1) * CHUNKS + RING))
                nc.scalar.activation(KT[:, h, 128 * c:128 * c + 128], kv_ps[:, 0:128], ACT.Copy).then_inc(kv_ready, 1)
                nc.scalar.activation(V[:, h, c, :], kv_ps[:, 128:256], ACT.Copy).then_inc(kv_ready, 1)

            def evac_attention(n, c, h):
                j = c * H + h
                act.wait_ge(pT_done, n * (C * H) + (j + 1))
                nc.scalar.activation(PT[:, 0:c + 1, :], pT_ps[:, 0:128 * (c + 1)].rearrange("p (a i) -> p a i", i=128),
                                     ACT.Copy).then_inc(pT_ready, 1)
                act.wait_ge(o_done, n * (C * H) + (j + 1))
                nc.scalar.activation(oT[:, :], o_ps[:, 0:128], ACT.Copy).then_inc(oT_ready, 1)

            def exponential(n, c, h):
                act.wait_ge(max_ready, n * (C * H) + (c * H + h + 1))
                nc.scalar.activation(P[:, h % 2, 0:128 * (c + 1)], score_ps[:, 0:128 * (c + 1)], ACT.Exp,
                                     bias=nmax[:, h % 2:h % 2 + 1],
                                     accum_out=rsum[:, h % 2:h % 2 + 1]).then_inc(exp_ready, 1)

            def evac_fill(n, c, f, dst, scale=1.0):
                act.wait_ge(fill_done, n * (8 * C) + (8 * c + f + 1))
                nc.scalar.activation(dst, fill[f % 2][:, :], ACT.Copy, scale=scale).then_inc(fill_ready, 1)

            def route(n, c, step, first=False):
                if step == 0:
                    if first:
                        recur(STEPS_LN)
                    act.wait_ge(mv_ready, n * 2 + (c + 1))
                    nc.scalar.activation(std[:, :], mv[:, 1:2], ACT.Sqrt, bias=eps[:, :]).then_inc(std_ready, 1)
                    act.wait_ge(lnT_done, n * 2 + (c + 1))
                    nc.scalar.activation(lnT[:, :], fill[1][:, 128:256], ACT.Copy).then_inc(lnT_ready, 1)
                    for f in range(2):
                        evac_fill(n, c, f, qpkT[:, 4 * f:4 * f + 4, :].rearrange("p a t -> p (a t)"))
                    for f in range(2):
                        evac_fill(n, c, 2 + f, qT[:, c, 4 * f:4 * f + 4, :].rearrange("p a t -> p (a t)"),
                                  float(D) ** -0.5)
                if step in (1, 2):
                    for hp in (2 * step - 2, 2 * step - 1):
                        evac_fill(n, c, 4 + hp, sims[:, hp].rearrange("p a b k -> p (a b k)"))
                if step == 3:
                    act.wait_ge(gaps, n * 2 + (c + 1))
                    nc.scalar.activation(wexp[:, :, :], wexp[:, :, :], ACT.Exp).then_inc(gexp, 1)

            def tile(n, c, nxt, plan=PLAN, first=False):
                for h in range(H):
                    if first:
                        recur(STEPS_CHUNK * CHUNKS)
                    evac_kv(n, c, h)
                    if h:
                        evac_attention(n, c, h - 1)
                    exponential(n, c, h)
                    if nxt is not None:
                        for step in plan[h]:
                            route(*nxt, step)
                evac_attention(n, c, H - 1)

            recur(STEPS_START)
            for step in range(3):
                route(0, 0, step, first=True)
            recur(STEPS - STEPS_START - STEPS_LN + STEPS_BEFORE // 2)
            route(0, 0, 3)
            recur(STEPS_BEFORE - STEPS_BEFORE // 2)
            tile(0, 0, (0, 1), FIRST_PLAN, first=True)
            with act.Fori(0, B - 1) as n:
                tile(n, 1, (n + 1, 0))
                tile(n + 1, 0, (n + 1, 1))
            tile(B - 1, 1, None)

        @block.tensor
        def _(pe):
            pe.wait_ge(const_landed, 64)
            pe.wait_ge(consts, 10)

            def transpose_x(i, g):
                pe.wait_ge(xn_ready, i * (2 * C * GROUPS) + (2 * C * (g + 1)))
                for r in range(2 * C):
                    last = nc.tensor.transpose(bank[0][:, 128 * r:128 * r + 128], xn_g[:, g % 2, r, :], ident[:, :])
                last.then_inc(xnT_done, 1)

            def beta(i, g):
                pe.wait_ge(lnTg_ready, i * GROUPS + (g + 1))
                for r in range(2 * C):
                    last = nc.tensor.matmul(bank[1][:, 128 * r:128 * r + 128], lnT_g[:, g % 2, r, :], we_sb[:, :],
                                            start=True, stop=True)
                last.then_inc(beta_done, 1)

            def graph_product(i, g):
                pe.wait_ge(agg_ready, i * GROUPS + (g + 1))
                pe.sem_inc(gate, 1)
                pe.wait_ge(betag_ready, i * (2 * C * GROUPS) + (2 * C * (g + 1)))
                for k in range(2):
                    for c in range(C):
                        last = nc.tensor.matmul(bank[2 + g % 2][:, L * k:L * k + L], beta_g[:, g % 2, C * k + c, :],
                                                adj_g[:, g, C * k + c, :], start=(c == 0), stop=(c == C - 1))
                last.then_inc(agg_done, 1)

            def turn(i, last=False):
                for g in range(GROUPS):
                    if g < GROUPS - 1 or not last:
                        ahead = (i, g + 1) if g < GROUPS - 1 else (i + 1, 0)
                        transpose_x(*ahead)
                    graph_product(i, g)
                    if g < GROUPS - 1 or not last:
                        beta(*ahead)

            transpose_x(0, 0)
            beta(0, 0)
            with pe.Fori(0, NG // GROUPS - 1) as i:
                turn(i)
            turn(NG // GROUPS - 1, last=True)

            def input_product(bank_no, block):
                nc.tensor.matmul(z_ps[bank_no][:, :], wx_sb[:, :],
                                 h_all[:, bass.ds(block * STEPS, STEPS), :].rearrange("p t b -> p (t b)"),
                                 start=True, stop=True)

            pe.wait_ge(agg_ready, NG + 2)
            input_product(0, 0)
            pe.sem_inc(h_ready, 1)
            with pe.Fori(0, BLOCKS // 4) as i:
                for k in range(2):
                    for s in range(STEPS):
                        pe.wait_ge(h_ready, i * (2 * STEPS) + (k * STEPS + s + 1))
                        nc.tensor.matmul(z_ps[k][:, B * s:B * s + B], wh_sb[:, :],
                                         h_ring[:, (k * STEPS + s - 1) % (2 * STEPS), :],
                                         start=False, stop=True, skip_group_check=True).then_inc(z_done, 1)
                        if s == 1:
                            input_product(1 - k, i * 2 + (k + 1))

            later_steps = iter(range(L // 2, L))

            def recur(count):
                for t in itertools.islice(later_steps, count):
                    b, s = divmod(t, STEPS)
                    pe.wait_ge(h_ready, t + 1)
                    nc.tensor.matmul(z_ps[b % 2][:, B * s:B * s + B], wh_sb[:, :],
                                     h_ring[:, 2 * STEPS - 1, :] if t == L // 2 else h_all[:, t - 1, :],
                                     start=False, stop=True, skip_group_check=True).then_inc(z_done, 1)
                    if s == 1 and BLOCKS // 2 < b < BLOCKS - 1:
                        input_product((b + 1) % 2, b + 1)

            pe.wait_ge(weights_landed, 7 * 16)
            pe.wait_ge(setup, 2)
            pe.sem_inc(ws_done, RING)
            pe.sem_inc(kv_ready, 2)
            pe.sem_inc(exp_ready, 1)
            pe.sem_inc(y_ready, 1)
            pe.sem_inc(fill_ready, 2)

            def weighted_sums(n, c, h, first=False):
                j = c * H + h
                pe.wait_ge(diag_ready, n * (C * H) + (j + 1))
                pe.sem_inc(gate, 1)
                pe.wait_ge(kv_ready, n * (2 * C * H) + (2 * j + 2))
                pe.sem_inc(gate, 1)
                for k in range(CHUNKS):
                    slot = (h % 2) * CHUNKS + k
                    pe.wait_ge(landed[slot], n * (C * H // 2 * SLOTS * 16) + (j // 2 + 1) * SLOTS * 16)
                    for s in range(k * SLOTS, k * SLOTS + SLOTS):
                        at = (h % 2) * TOP + s
                        nc.tensor.matmul(kv_ps[:, 0:128], G[:, at, 0:D], diag[:, h % 2, s, :],
                                         start=(s == 0), stop=(s == TOP - 1), skip_group_check=True)
                        if first:
                            recur(1)
                        last = nc.tensor.matmul(kv_ps[:, 128:256], diag[:, h % 2, s, :], G[:, at, D:2 * D],
                                                start=False, stop=(s == TOP - 1), skip_group_check=True)
                        if first and s % SLOTS < STEPS_CHUNK - SLOTS:
                            recur(1)
                    last.then_inc(ws_done, 1)

            def scores(n, c, h):
                j = c * H + h
                pe.wait_ge(exp_ready, n * (C * H) + (j + 1))
                own = score_ps[:, 128 * c:128 * c + 128]
                nc.tensor.matmul(own, identb[:, :], maskb[:, :], start=True, stop=False)
                pe.wait_ge(kv_ready, n * (2 * C * H) + (2 * j + 4))
                last = nc.tensor.matmul(own, qT[:, c, h, :], KT[:, h, 128 * c:128 * c + 128], start=False, stop=True)
                if c:
                    last = nc.tensor.matmul(score_ps[:, 0:128], qT[:, c, h, :], KT[:, h, 0:128], start=True, stop=True)
                last.then_inc(scores_done, 1)

            def attention(n, c, h):
                j = c * H + h
                pe.wait_ge(p_ready, n * (C * H) + (j + 1))
                for a in range(c + 1):
                    last = nc.tensor.transpose(pT_ps[:, 128 * a:128 * a + 128], P[:, h % 2, 128 * a:128 * a + 128],
                                               ident[:, :])
                last.then_inc(pT_done, 1)
                pe.wait_ge(pT_ready, n * (C * H) + (j + 1))
                for a in range(c + 1):
                    last = nc.tensor.matmul(o_ps[:, 0:128], V[:, h, a, :], PT[:, a, :], start=(a == 0), stop=(a == c))
                last.then_inc(o_done, 1)
                if h == 0:
                    pe.wait_ge(y_ready, n * 2 + (c + 1))
                    pe.sem_inc(gate, 1)
                pe.wait_ge(oT_ready, n * (C * H) + (j + 1))
                last = nc.tensor.matmul(wo_ps[:, 0:128], oT[:, :], wo_sb[:, h, :], start=(h == 0), stop=(h == H - 1))
                if h == H - 1:
                    last.then_inc(wo_done, 1)

            def fill_bank(n, c, f, products):
                pe.wait_ge(fill_ready, n * (8 * C) + (8 * c + f + 1))
                for at, lhsT, rhs in products:
                    last = nc.tensor.matmul(fill[f % 2][:, at], lhsT, rhs, start=True, stop=True)
                last.then_inc(fill_done, 1)

            def route(n, c, step, first=False):
                if step == 0:
                    pe.wait_ge(fill_ready, n * (8 * C) + (8 * c + 2))
                    pe.sem_inc(gate, 1)
                    pe.wait_ge(yT_ready, n * 2 + (c + 1))
                    nc.tensor.transpose(fill[1][:, 0:128], yT[:, :], ident[:, :]).then_inc(yback_done, 1)
                    if first:
                        recur(STEPS_LN)
                    pe.wait_ge(ln_ready, n * 2 + (c + 1))
                    nc.tensor.transpose(fill[1][:, 128:256], ln[:, :], ident[:, :]).then_inc(lnT_done, 1)
                    pe.wait_ge(lnT_ready, n * 2 + (c + 1))
                    for f in range(2):
                        fill_bank(n, c, f, [(slice(128 * a, 128 * a + 128), wqpk_sb[:, 4 * f + a, :], lnT[:, :])
                                            for a in range(4)])
                    for f in range(2):
                        fill_bank(n, c, 2 + f, [(slice(128 * a, 128 * a + 128), wq_sb[:, 4 * f + a, :], lnT[:, :])
                                                for a in range(4)])
                if step in (1, 2):
                    for hp in (2 * step - 2, 2 * step - 1):
                        fill_bank(n, c, 4 + hp, [(slice(256 * half, 256 * half + 256), qpkT[:, 4 * half + hp, :],
                                                  keys_bd[:, half, hp, :, :].rearrange("p a k -> p (a k)"))
                                                 for half in range(2)])

            def tile(n, c, nxt, plan=PLAN, first=False):
                for h in range(H):
                    weighted_sums(n, c, h, first)
                    scores(n, c, h)
                    if h:
                        attention(n, c, h - 1)
                    if nxt is not None:
                        if first and 0 in plan[h]:
                            pe.wait_ge(h_ready, L + 1)
                            pe.sem_inc(gate, 1)
                        for step in plan[h]:
                            route(*nxt, step)
                attention(n, c, H - 1)

            recur(STEPS_START)
            for step in range(3):
                route(0, 0, step, first=True)
            recur(STEPS - STEPS_START - STEPS_LN)
            pe.wait_ge(fill_ready, 8 + 2)
            input_product(1, BLOCKS // 2 + 1)
            recur(STEPS_BEFORE)
            tile(0, 0, (0, 1), FIRST_PLAN, first=True)
            with pe.Fori(0, B - 1) as n:
                tile(n, 1, (n + 1, 0))
                tile(n + 1, 0, (n + 1, 1))
            tile(B - 1, 1, None)

        @block.vector
        def _(dve):
            chain = Count()

            def follow():
                dve.wait_ge(v_chain, chain.value)

            def clear_chain():
                follow()
                dve.sem_clear(v_chain)
                chain.value = 0

            dve.wait_ge(consts, 6)
            nc.vector.tensor_copy(rowbase[:, :, :].rearrange("p h k -> p (h k)"), iota_i[:, :]).then_inc(bases_read, 1)
            nc.vector.memset(keys_bd[:, 0, :, :, :], 0.0).then_inc(setup, 1)
            nc.vector.memset(keys_bd[:, 1, :, :, :], 0.0).then_inc(setup, 1)
            dve.wait_ge(consts, 10)
            dve.wait_ge(ident_copied, 1)
            nc.vector.tensor_copy(iota_ps, iota_i[:, 0:NC]).then_inc(v_chain, 1)
            chain.up()

            def tile_stats(i, rows):
                for r in rows:
                    nc.vector.bn_stats(x_stats[:, r, :],
                                       x_all[:, bass.ds(i * 16 + r, 1), :].rearrange("p r d -> p (r d)")
                                       ).then_inc(v_chain, 1)
                    chain.up()

            def turn_stats(i):
                follow()
                mean_even, mean_odd = x_stats[:, :, 1], x_stats[:, :, 4]
                nc.vector.tensor_tensor(dmean[:, :], mean_even, mean_odd, ALU.subtract).then_inc(v_chain, 1)
                nc.vector.tensor_tensor(vsum[:, :], x_stats[:, :, 2], x_stats[:, :, 5], ALU.add).then_inc(v_chain, 1)
                nc.vector.tensor_tensor(mean[:, 1, :], mean_even, mean_odd, ALU.add).then_inc(v_chain, 1)
                chain.value += 3
                follow()
                nc.vector.tensor_tensor(dmean[:, :], dmean[:, :], dmean[:, :], ALU.mult).then_inc(v_chain, 1)
                chain.up()
                nc.vector.tensor_scalar(mean[:, 1, :], mean[:, 1, :], 0.5, None, ALU.mult).then_inc(v_chain, 1)
                chain.up()
                follow()
                nc.vector.scalar_tensor_tensor(vsum[:, :], dmean[:, :], D / 4.0, vsum[:, :],
                                               ALU.mult, ALU.add).then_inc(vars_ready, 1)

            def take_stats(i):
                dve.wait_ge(std_all, i + 1)
                nc.vector.reciprocal(rstd[:, 1, :], rstd[:, 0, :]).then_inc(v_chain, 1)
                chain.up()
                nc.vector.tensor_copy(mean[:, 0, :], mean[:, 1, :]).then_inc(v_chain, 1)
                chain.up()
                follow()

            def normalise_group(i, g):
                for r in range(2 * C):
                    at = 4 * g + r
                    nc.vector.tensor_scalar(
                        xn_g[:, g % 2, r, :], x_all[:, bass.ds(i * 16 + at, 1), :].rearrange("p r d -> p (r d)"),
                        mean[:, 0, at:at + 1], rstd[:, 1, at:at + 1],
                        ALU.subtract, ALU.mult).then_inc(xn_ready, 1)
                dve.wait_ge(adj_landed[g], i * 32 + 32)
                nc.vector.reduce_sum(norm_g[:, g % 2, :], adj_g[:, g, :, :], axis=X).then_inc(v_chain, 1)
                chain.up()
                follow()
                nc.vector.tensor_scalar(norm_g[:, g % 2, :], norm_g[:, g % 2, :], EPS_NORM, None,
                                        ALU.max).then_inc(v_chain, 1)
                chain.up()
                follow()
                nc.vector.reciprocal(rnorm_g[:, g % 2, :], norm_g[:, g % 2, :]).then_inc(norm_ready, 1)

            def turn(i, last=False):
                for g in range(GROUPS):
                    if g < GROUPS - 1:
                        if not last:
                            tile_stats(i + 1, range(8 * g, 8 * g + 8) if g < 2 else ())
                            if g == 1:
                                turn_stats(i + 1)
                        dve.wait_ge(agg_done, i * GROUPS + (g + GROUPS))
                        dve.sem_inc(gate, 1)
                        normalise_group(i, g + 1)
                    elif not last:
                        dve.wait_ge(agg_done, i * GROUPS + (g + GROUPS))
                        dve.sem_inc(gate, 1)
                        take_stats(i + 1)
                        normalise_group(i + 1, 0)

            dve.wait_ge(x_first, 16)
            tile_stats(0, range(16))
            turn_stats(0)
            take_stats(0)
            normalise_group(0, 0)
            clear_chain()
            dve.wait_ge(x_rest, 16 * (B // X_TURN - 1))
            with dve.Fori(0, NG // GROUPS - 1) as i:
                turn(i)
                clear_chain()
            turn(NG // GROUPS - 1, last=True)
            clear_chain()

            with dve.Fori(0, BLOCKS // 4) as i:
                for k in range(2):
                    dve.wait_ge(h_ready, i * (2 * STEPS) + (k + 1) * STEPS + 1)
                    dve.sem_inc(gate, 1)
                    nc.vector.tensor_copy(
                        h_all[:, bass.ds(i * (2 * STEPS) + k * STEPS, STEPS), :],
                        h_ring[:, k * STEPS:k * STEPS + STEPS, :]).then_inc(h_copied, 1)
            dve.wait_ge(h_copied, BLOCKS // 2 + 2)
            for c in range(C):
                dve.sem_inc(stored[c], 16)

            def diagonal(n, c, h):
                dve.wait_ge(ws_done, n * (C * H * CHUNKS) + ((c * H + h - 1) * CHUNKS + RING))
                dve.sem_inc(gate, 1)
                nc.vector.tensor_tensor(diag[:, h % 2, :, :],
                                        ident_ps.unsqueeze(1).broadcast_to([128, TOP, 128]),
                                        w[:, c, h, :].unsqueeze(2).broadcast_to([128, TOP, 128]),
                                        ALU.mult).then_inc(diag_ready, 1)

            def row_max(n, c, h):
                dve.wait_ge(scores_done, n * (C * H) + (c * H + h + 1))
                nc.vector.tensor_reduce(nmax[:, h % 2:h % 2 + 1], score_ps[:, 0:128 * (c + 1)], axis=X, op=ALU.max,
                                        negate=True).then_inc(max_ready, 1)

            def normalise(n, c, h):
                dve.wait_ge(exp_ready, n * (C * H) + (c * H + h + 2))
                nc.vector.reciprocal(rrec[:, h % 2:h % 2 + 1], rsum[:, h % 2:h % 2 + 1]).then_inc(v_chain, 1)
                chain.up()
                follow()
                nc.vector.tensor_scalar(P[:, h % 2, 0:128 * (c + 1)], P[:, h % 2, 0:128 * (c + 1)],
                                        rrec[:, h % 2:h % 2 + 1], None, ALU.mult).then_inc(p_ready, 1)

            def top16(jobs):
                marks = []
                for src, _, best, _ in jobs:
                    nc.vector.max(best[:, 0:8], src).then_inc(v_chain, 1)
                    marks.append(chain.up())
                for j, (src, rest, best, at) in enumerate(jobs):
                    dve.wait_ge(v_chain, marks[j])
                    nc.vector.match_replace(rest, best[:, 0:8], src, REPLACED).then_inc(v_chain, 1)
                    marks[j] = chain.up()
                    nc.vector.max_index(at[:, 0:8], best[:, 0:8], src).then_inc(v_chain, 1)
                    chain.up()
                for j, (_, rest, best, _) in enumerate(jobs):
                    dve.wait_ge(v_chain, marks[j])
                    nc.vector.max(best[:, 8:16], rest).then_inc(v_chain, 1)
                    marks[j] = chain.up()
                for j, (_, rest, best, at) in enumerate(jobs):
                    dve.wait_ge(v_chain, marks[j])
                    nc.vector.max_index(at[:, 8:16], best[:, 8:16], rest).then_inc(v_chain, 1)
                    chain.up()

            def layernorm(n, c):
                nc.vector.tensor_copy(yT[:, :], h_all[:, 128 * c:128 * c + 128, bass.ds(n, 1)]
                                      .rearrange("p t b -> p (t b)")).then_inc(yT_ready, 1)
                dve.wait_ge(yback_done, n * 2 + (c + 1))
                dve.sem_inc(gate, 1)
                nc.vector.tensor_tensor(x1[:, c, :], x_all[:, bass.ds(n * 2 + c, 1), :].rearrange("p r d -> p (r d)"),
                                        fill[1][:, 0:128], ALU.add).then_inc(v_chain, 1)
                chain.up()
                follow()
                nc.vector.bn_stats(stats[:, :], x1[:, c, :]).then_inc(v_chain, 1)
                chain.up()
                follow()
                nc.vector.bn_aggr(mv[:, :], stats[:, :]).then_inc(mv_ready, 1)
                dve.wait_ge(std_ready, n * 2 + (c + 1))
                nc.vector.reciprocal(rs[:, :], std[:, :]).then_inc(v_chain, 1)
                chain.up()
                follow()
                nc.vector.tensor_scalar(ln[:, :], x1[:, c, :], mv[:, 0:1], rs[:, :],
                                        ALU.subtract, ALU.mult).then_inc(ln_ready, 1)

            def half_keys(n, c, step):
                for hp in (2 * step - 2, 2 * step - 1):
                    dve.wait_ge(fill_ready, n * (8 * C) + (8 * c + 4 + hp + 3))
                    dve.sem_inc(gate, 1)
                    top16([(sims[:, hp, half, hh, :], spare[:, 2 * half + hh, :], S1[:, half, 2 * hp + hh, :],
                            I1[:, half, 2 * hp + hh, :]) for half in range(2) for hh in range(2)])

            def pairs(n, c):
                follow()
                nc.vector.tensor_tensor(I1f[:, 0], I1[:, 0], rowbase[:, :, :], ALU.add).then_inc(v_chain, 1)
                chain.up()
                nc.vector.tensor_scalar(I1f[:, 1], I1[:, 1], float(NK), None, ALU.mult).then_inc(v_chain, 1)
                chain.up()
                for dst, src in ((CV, S1), (CI, I1f)):
                    at = 0
                    if src is I1f:
                        follow()
                    for i0, ni, nj in PAIRS:
                        if ni == 1:
                            shape = [128, H, nj]
                            o = dst[:, :, at:at + nj]
                            a, b = src[:, 0, :, i0:i0 + 1].broadcast_to(shape), src[:, 1, :, 0:nj]
                        elif nj == 1:
                            shape = [128, H, ni]
                            o = dst[:, :, at:at + ni]
                            a, b = src[:, 0, :, i0:i0 + ni], src[:, 1, :, 0:1].broadcast_to(shape)
                        else:
                            shape = [128, H, ni, nj]
                            o = dst[:, :, at:at + ni * nj].rearrange("p h (i j) -> p h i j", j=nj)
                            a = src[:, 0, :, i0:i0 + ni].unsqueeze(3).broadcast_to(shape)
                            b = src[:, 1, :, 0:nj].unsqueeze(2).broadcast_to(shape)
                        nc.vector.tensor_tensor(o, a, b, ALU.add).then_inc(v_chain, 1)
                        chain.up()
                        at += ni * nj
                follow()
                for h0 in (0, 4):
                    top16([(CV[:, h, :], spare[:, h - h0, 0:NC], S2[:, h, :], P2[:, h, :])
                           for h in range(h0, h0 + 4)])
                follow()
                nc.vector.tensor_copy(P2f[:, :, :], P2[:, :, :]).then_inc(v_chain, 1)
                chain.up()
                nc.vector.tensor_tensor(wexp[:, :, :], S2[:, :, :], S2[:, :, 0:1].broadcast_to([128, H, TOP]),
                                        ALU.subtract).then_inc(gaps, 1)

            def table_rows(n, c, h0):
                hs = slice(h0, h0 + 2)
                shape = [128, 2, TOP, NC]
                follow()
                nc.vector.tensor_copy(CI_ps, CI[:, hs, :]).then_inc(v_chain, 1)
                chain.up()
                nc.vector.tensor_tensor(
                    hot[:, :, :, :], P2f[:, hs, :].unsqueeze(3).broadcast_to(shape),
                    iota_ps.unsqueeze(1).unsqueeze(1).broadcast_to(shape), ALU.is_equal).then_inc(v_chain, 1)
                chain.up()
                follow()
                nc.vector.tensor_tensor(hot[:, :, :, :], hot[:, :, :, :],
                                        CI_ps.unsqueeze(2).broadcast_to(shape), ALU.mult).then_inc(v_chain, 1)
                chain.up()
                follow()
                nc.vector.reduce_sum(rowf[:, hs, :], hot[:, :, :, :], axis=X).then_inc(v_chain, 1)
                chain.up()
                follow()
                nc.vector.tensor_copy(idx[:, c, TOP * h0:TOP * h0 + 2 * TOP],
                                      rowf[:, hs, :].rearrange("p h k -> p (h k)")).then_inc(idx_ready, 1)

            def weights(n, c):
                dve.wait_ge(gexp, n * 2 + (c + 1))
                nc.vector.reduce_sum(wsum[:, :], wexp[:, :, :], axis=X).then_inc(v_chain, 1)
                chain.up()
                follow()
                nc.vector.reciprocal(wsum[:, :], wsum[:, :]).then_inc(v_chain, 1)
                chain.up()
                follow()
                nc.vector.tensor_tensor(w[:, c, :, :], wexp[:, :, :],
                                        wsum[:, :].unsqueeze(2).broadcast_to([128, H, TOP]),
                                        ALU.mult).then_inc(v_chain, 1)
                chain.up()

            def route(n, c, step):
                if step == 0:
                    layernorm(n, c)
                if step in (1, 2):
                    half_keys(n, c, step)
                if step == 3:
                    pairs(n, c)
                    weights(n, c)
                if step in (4, 5):
                    for h0 in (4 * step - 16, 4 * step - 14):
                        table_rows(n, c, h0)

            def tile(n, c, nxt, plan=PLAN, first=False):
                for h in range(H):
                    if h:
                        normalise(n, c, h - 1)
                    if h < H - 1:
                        diagonal(n, c, h + 1)
                    elif nxt is not None and not first:
                        diagonal(*nxt, 0)
                    row_max(n, c, h)
                    if nxt is not None:
                        if first and 0 in plan[h]:
                            dve.wait_ge(h_ready, L + 1)
                        for step in plan[h]:
                            route(*nxt, step)
                normalise(n, c, H - 1)
                if first:
                    diagonal(*nxt, 0)
                dve.wait_ge(stored[c], n * 16 + 16)
                dve.sem_inc(gate, 1)
                dve.wait_ge(wo_done, n * 2 + (c + 1))
                nc.vector.tensor_tensor(y[:, c, :], x1[:, c, :], wo_ps[:, 0:128], ALU.add).then_inc(y_ready, 1)
                clear_chain()

            for step in range(4):
                route(0, 0, step)
            table_rows(0, 0, 0)
            diagonal(0, 0, 0)
            for h0 in (2, 4, 6):
                table_rows(0, 0, h0)
            clear_chain()
            tile(0, 0, (0, 1), FIRST_PLAN, first=True)
            with dve.Fori(0, B - 1) as n:
                tile(n, 1, (n + 1, 0))
                tile(n + 1, 0, (n + 1, 1))
            tile(B - 1, 1, None)


_ORDER = ["x", "adj", "L0_gnn_e_weight", "L0_gnn_Wx", "L0_gnn_Wh", "L0_gnn_b", "L0_ffn_Wq_pk",
          "pk_keys_t", "L0_ffn_Wq", "key_value_rows", "L0_ffn_Wo"]


def kernel(**inputs):
    import numpy as _np
    import concourse.bacc as _bacc
    from concourse import mybir as _mybir
    from concourse.bass_utils import run_bass_kernel_spmd as _run

    arrays = {k: _np.asarray(v) for k, v in inputs.items()}
    keys = arrays.pop("L0_ffn_pk_keys").transpose(2, 3, 0, 1).reshape(H // 2, 2 * DK, 2, NK)
    arrays["pk_keys_t"] = _np.ascontiguousarray(keys.transpose(1, 2, 0, 3))
    arrays["key_value_rows"] = _np.concatenate(
        [arrays.pop("L0_ffn_keys_table"), arrays.pop("L0_ffn_values_table")], axis=1)

    nc = _bacc.Bacc("TRN2", target_bir_lowering=False, num_devices=1)
    feeds, args = {}, []
    for name in _ORDER:
        a = _np.ascontiguousarray(arrays[name])
        feeds[f"in_{name}"] = a
        args.append(nc.dram_tensor(f"in_{name}", a.shape, _mybir.dt.from_np(a.dtype), kind="ExternalInput").ap())
    args.append(nc.dram_tensor("out_x", (B, L, D), _mybir.dt.float32, kind="ExternalOutput").ap())
    build(nc, *args)
    return _run(nc, [feeds], core_ids=[0]).results[0]["out_x"]
```
